# Optimizing a Trainium2 kernel written in Bass

```python
import numpy as np
import jax
import jax.numpy as jnp

def _softmax(x, axis=-1):
    return jax.nn.softmax(x, axis=axis)

def _gelu(x):
    return jax.nn.gelu(x, approximate=True)

def _silu(x):
    return jax.nn.silu(x)

def _sigmoid(x):
    return jax.nn.sigmoid(x)

def _layernorm(x, axis=-1, eps=1e-05):
    m = jnp.mean(x, axis=axis, keepdims=True)
    v = jnp.var(x, axis=axis, keepdims=True)
    return (x - m) / jnp.sqrt(v + eps)

def _scatter_add(tgt, idx, src, axis=0):
    return tgt.at[idx].add(src)

def _segment_sum(src, seg, n):
    return jax.ops.segment_sum(src, seg, n)
kernel_name = 'mk_conv_seq_d2_conv_nhwc128_r4_410a8e'

def setup_inputs(seed: int=0):
    np.random.seed(seed)
    _w = jnp.asarray

    def _rec_inputs():
        import jax
        import jax.numpy as jnp
        _gk = jax.random.key(seed)
        x = -0.000125 + 0.9999 * jax.random.normal(jax.random.fold_in(_gk, 1), (1, 128, 128, 32), jnp.float32)
        return x
    x = _rec_inputs()

    def _L0_conv_setup():
        import jax, jax.numpy as jnp
        import numpy as np
        EPS = 1e-05

        def _layernorm(x, w, b):
            m = jnp.mean(x, axis=-1, keepdims=True)
            v = jnp.mean(jnp.square(x - m), axis=-1, keepdims=True)
            return (x - m) * jax.lax.rsqrt(v + EPS) * w + b
        key = jax.random.key(seed)
        ks = jax.random.split(key, 8)
        N, S, Z, E = (1, 128, 32, 32)
        scale = 0.02
        return {'pair_repr': jax.random.normal(ks[0], (N, S, S, Z), dtype=jnp.float32), 'ln1_w': jnp.ones((Z,), jnp.float32), 'ln1_b': jnp.zeros((Z,), jnp.float32), 'left1': jax.random.normal(ks[1], (Z, E), jnp.float32) * scale, 'left2': jax.random.normal(ks[2], (Z, E), jnp.float32) * scale, 'right1': jax.random.normal(ks[3], (Z, E), jnp.float32) * scale, 'right2': jax.random.normal(ks[4], (Z, E), jnp.float32) * scale, 'ln2_w': jnp.ones((E,), jnp.float32), 'ln2_b': jnp.zeros((E,), jnp.float32), 'out_w': jax.random.normal(ks[5], (E, Z), jnp.float32) * scale, 'gate': jax.random.normal(ks[6], (Z, Z), jnp.float32) * scale}
    _L0_conv_all = _L0_conv_setup()
    _L0_conv_in = {k: v for k, v in _L0_conv_all.items() if k in ('ln1_w', 'ln1_b', 'left1', 'left2', 'right1', 'right2', 'ln2_w', 'ln2_b', 'out_w', 'gate')}
    del _L0_conv_all

    def _L1_conv_setup():
        import jax, jax.numpy as jnp
        import numpy as np
        LN_EPS = 1e-05

        def _layer_norm(x, scale, bias):
            mu = jnp.mean(x, axis=-1, keepdims=True)
            var = jnp.mean(jnp.square(x - mu), axis=-1, keepdims=True)
            return (x - mu) * jax.lax.rsqrt(var + LN_EPS) * scale + bias
        key = jax.random.key(seed)
        ks = jax.random.split(key, 8)
        B, N, C, H = (1, 96, 32, 32)
        s_in = 1.0 / np.sqrt(C)
        s_h = 1.0 / np.sqrt(H)
        return {'pair': jax.random.normal(ks[0], (B, N, N, C), jnp.float32), 'W_left': jax.random.normal(ks[1], (C, H), jnp.float32) * s_in, 'b_left': jnp.zeros((H,), jnp.float32), 'W_right': jax.random.normal(ks[2], (C, H), jnp.float32) * s_in, 'b_right': jnp.zeros((H,), jnp.float32), 'W_gate': jax.random.normal(ks[3], (C, H), jnp.float32) * s_in, 'b_gate': jnp.zeros((H,), jnp.float32), 'W_eq': jax.random.normal(ks[4], (C, H), jnp.float32) * s_in, 'b_eq': jnp.zeros((H,), jnp.float32), 'W_out': jax.random.normal(ks[5], (H, C), jnp.float32) * s_h, 'b_out': jnp.zeros((C,), jnp.float32), 'ln_scale': jnp.ones((C,), jnp.float32), 'ln_bias': jnp.zeros((C,), jnp.float32)}
    _L1_conv_all = _L1_conv_setup()
    _L1_conv_in = {k: v for k, v in _L1_conv_all.items() if k in ('W_left', 'b_left', 'W_right', 'b_right', 'W_gate', 'b_gate', 'W_eq', 'b_eq', 'W_out', 'b_out', 'ln_scale', 'ln_bias')}
    del _L1_conv_all
    return {'x': x, 'L0_conv_ln1_w': _L0_conv_in['ln1_w'], 'L0_conv_ln1_b': _L0_conv_in['ln1_b'], 'L0_conv_left1': _L0_conv_in['left1'], 'L0_conv_left2': _L0_conv_in['left2'], 'L0_conv_right1': _L0_conv_in['right1'], 'L0_conv_right2': _L0_conv_in['right2'], 'L0_conv_ln2_w': _L0_conv_in['ln2_w'], 'L0_conv_ln2_b': _L0_conv_in['ln2_b'], 'L0_conv_out_w': _L0_conv_in['out_w'], 'L0_conv_gate': _L0_conv_in['gate'], 'L1_conv_W_left': _L1_conv_in['W_left'], 'L1_conv_b_left': _L1_conv_in['b_left'], 'L1_conv_W_right': _L1_conv_in['W_right'], 'L1_conv_b_right': _L1_conv_in['b_right'], 'L1_conv_W_gate': _L1_conv_in['W_gate'], 'L1_conv_b_gate': _L1_conv_in['b_gate'], 'L1_conv_W_eq': _L1_conv_in['W_eq'], 'L1_conv_b_eq': _L1_conv_in['b_eq'], 'L1_conv_W_out': _L1_conv_in['W_out'], 'L1_conv_b_out': _L1_conv_in['b_out'], 'L1_conv_ln_scale': _L1_conv_in['ln_scale'], 'L1_conv_ln_bias': _L1_conv_in['ln_bias']}

def reference(x, L0_conv_ln1_w, L0_conv_ln1_b, L0_conv_left1, L0_conv_left2, L0_conv_right1, L0_conv_right2, L0_conv_ln2_w, L0_conv_ln2_b, L0_conv_out_w, L0_conv_gate, L1_conv_W_left, L1_conv_b_left, L1_conv_W_right, L1_conv_b_right, L1_conv_W_gate, L1_conv_b_gate, L1_conv_W_eq, L1_conv_b_eq, L1_conv_W_out, L1_conv_b_out, L1_conv_ln_scale, L1_conv_ln_bias):
    import jax
    import jax.numpy as jnp

    def _L0_conv_ref(pair_repr, ln1_w, ln1_b, left1, left2, right1, right2, ln2_w, ln2_b, out_w, gate):
        import jax, jax.numpy as jnp
        import numpy as np
        EPS = 1e-05

        def _layernorm(x, w, b):
            m = jnp.mean(x, axis=-1, keepdims=True)
            v = jnp.mean(jnp.square(x - m), axis=-1, keepdims=True)
            return (x - m) * jax.lax.rsqrt(v + EPS) * w + b
        residual = pair_repr
        x = _layernorm(pair_repr, ln1_w, ln1_b)
        left = jax.nn.sigmoid(x @ left1) * (x @ left2)
        right = jax.nn.sigmoid(x @ right1) * (x @ right2)
        p = jnp.einsum('nsre,nkre->nske', left, right)
        p = _layernorm(p, ln2_w, ln2_b)
        g = jax.nn.sigmoid(jnp.einsum('nsrz,zy->nsry', x, gate))
        q = jnp.einsum('nrse,ez->nsrz', p, out_w) * g
        return residual + q

    def _L1_conv_ref(pair, W_left, b_left, W_right, b_right, W_gate, b_gate, W_eq, b_eq, W_out, b_out, ln_scale, ln_bias):
        import jax, jax.numpy as jnp
        import numpy as np
        LN_EPS = 1e-05

        def _layer_norm(x, scale, bias):
            mu = jnp.mean(x, axis=-1, keepdims=True)
            var = jnp.mean(jnp.square(x - mu), axis=-1, keepdims=True)
            return (x - mu) * jax.lax.rsqrt(var + LN_EPS) * scale + bias
        left = pair @ W_left + b_left
        right = pair @ W_right + b_right
        gate = jax.nn.sigmoid(pair @ W_gate + b_gate)
        left = left + (pair @ W_eq + b_eq)
        right_sum = jnp.sum(right, axis=2, keepdims=True)
        out = left * right_sum
        out = out * gate
        out = out @ W_out + b_out
        return _layer_norm(out + pair, ln_scale, ln_bias)

    def _gn(v, G=32, eps=1e-05):
        B_, H_, W_, C_ = v.shape
        g = v.reshape(B_, H_, W_, G, C_ // G)
        m = jnp.mean(g, axis=(1, 2, 4), keepdims=True)
        s = jnp.var(g, axis=(1, 2, 4), keepdims=True)
        return ((g - m) / jnp.sqrt(s + eps)).reshape(v.shape)

    def _ln_c(v, eps=1e-06):
        m = jnp.mean(v, axis=-1, keepdims=True)
        s = jnp.var(v, axis=-1, keepdims=True)
        return (v - m) / jnp.sqrt(s + eps)

    def _ln_t(v, eps=1e-05):
        m = jnp.mean(v, axis=-1, keepdims=True)
        s = jnp.var(v, axis=-1, keepdims=True)
        return (v - m) / jnp.sqrt(s + eps)

    def _to_tokens(v):
        B_, H_, W_, C_ = v.shape
        return v.reshape(B_, H_ * W_, C_)

    def _from_tokens(t, like):
        return t.reshape(like.shape)
    x = _L0_conv_ref(x, L0_conv_ln1_w, L0_conv_ln1_b, L0_conv_left1, L0_conv_left2, L0_conv_right1, L0_conv_right2, L0_conv_ln2_w, L0_conv_ln2_b, L0_conv_out_w, L0_conv_gate)
    x = _L1_conv_ref(x, L1_conv_W_left, L1_conv_b_left, L1_conv_W_right, L1_conv_b_right, L1_conv_W_gate, L1_conv_b_gate, L1_conv_W_eq, L1_conv_b_eq, L1_conv_W_out, L1_conv_b_out, L1_conv_ln_scale, L1_conv_ln_bias)
    return x

_drawn_inputs = setup_inputs


def setup_inputs(seed=0):
    import zlib

    import numpy as np

    out = dict(_drawn_inputs(seed))
    spreads = {'L0_conv_ln1_w': (1.0, 0.57),
     'L0_conv_ln1_b': (0.0, 0.1),
     'L0_conv_ln2_w': (1.0, 0.6),
     'L0_conv_ln2_b': (0.0, 0.1),
     'L1_conv_b_left': (0.0, 0.1),
     'L1_conv_b_right': (0.0, 0.1),
     'L1_conv_b_gate': (0.0, 0.27),
     'L1_conv_b_eq': (0.0, 0.1),
     'L1_conv_b_out': (0.0, 0.8),
     'L1_conv_ln_scale': (1.0, 0.2),
     'L1_conv_ln_bias': (0.0, 0.1)}
    factors = {'L0_conv_left1': 5.885, 'L0_conv_right1': 8.0, 'L0_conv_gate': 8.0}
    for name, (base, spread) in spreads.items():
        noise = np.random.default_rng([zlib.crc32(name.encode()), seed]).standard_normal(out[name].shape)
        drawn = base * np.exp(spread * noise) if base else spread * noise
        out[name] = jnp.asarray(drawn.astype(out[name].dtype))
    for name, factor in factors.items():
        out[name] = (out[name] * factor).astype(out[name].dtype)
    return out
```

```python
import concourse.bass as bass
from concourse import mybir
from contextlib import ExitStack

P = 128
CH = 32
GRP = P // CH
CHUNKS = 8
SPC = P // CHUNKS
COLS = SPC * CH
BLK = COLS // P
EPS = 1e-5
RSQRT_MAGIC = 0x5F3759DF

MATS = ["left1", "right1", "left2", "right2", "gate0", "out0", "wleft", "weq", "wgate", "wright", "wout"]
VECS = ["ln1_w", "ln1_b", "ln2_w", "ln2_b", "b_left", "b_eq", "b_right", "b_gate"]
ROWS = ["ln_scale", "ln_bias", "b_out"]

LN1 = [(0, 1), (1, 2), (2, 4), (4, 6), (6, 8)]
LN3 = [(0, 2), (2, 4), (4, 6), (6, 7), (7, 8)]


def pair_layers(nc, x, weights, rows, out):
    fp32, bf16, i32 = mybir.dt.float32, mybir.dt.bfloat16, mybir.dt.int32
    ALU, ACT, AX = mybir.AluOpType, mybir.ActivationFunctionType, mybir.AxisListType

    x_tok_dram = x[0].rearrange("s r c -> r s c")
    out_tok_dram = out[0].rearrange("s r c -> r s c")
    n_w = weights.shape[1]

    with ExitStack() as ctx:
        def sb(name, shape, dt=fp32):
            return ctx.enter_context(nc.sbuf_tensor(name, shape, dt))

        def sem(name):
            return ctx.enter_context(nc.semaphore(name))

        w_rep = sb("w_rep", [P, n_w])
        row_rep = sb("row_rep", [P, len(ROWS), CH])
        mask = sb("mask", [P, GRP, CH])
        ident = sb("ident", [P, P])
        center_blk = sb("center_blk", [P, P])
        lr_blk = sb("lr_blk", [P, GRP, 4, CH])
        gate0_blk = sb("gate0_blk", [P, P])
        out0_raw_blk = sb("out0_raw_blk", [P, P])
        out0_scaled = sb("out0_scaled", [P, CH])
        out0_blk = sb("out0_blk", [P, P])
        q_bias = sb("q_bias", [P, 1])
        leq = sb("leq", [P, CH])
        leq_blk = sb("leq_blk", [P, P])
        leq_bias = sb("leq_bias", [P, 1])
        gate1_blk = sb("gate1_blk", [P, P])
        right_blk = sb("right_blk", [P, P])
        right_bias = sb("right_bias", [P, 1])
        wout_mean = sb("wout_mean", [P, 1])
        wout_c = sb("wout_c", [P, CH])
        wout_blk = sb("wout_blk", [P, P])
        bo_mean = sb("bo_mean", [P, 1])
        bo_c = sb("bo_c", [P, 3, CH])
        bo_part = sb("bo_part", [P, 3, CH], bf16)
        bo_rows = sb("bo_rows", [P, SPC, CH], bf16)
        ones_rows = sb("ones_rows", [P, P], bf16)

        x_tok = sb("x_tok", [P, P, CH])
        xc = sb("xc", [P, P, CH])
        sq = sb("sq", [P, P, CH])
        xnT = sb("xnT", [P, CHUNKS, COLS])
        sig_lr = sb("sig_lr", [P, 3, 2 * COLS // 2])
        lr = sb("lr", [P, 2 * CH, P])
        p_sb = sb("p_sb", [P, CH, P])
        p_sq = sb("p_sq", [P, CH, P])
        acc_p = sb("acc_p", [P, 4, P])
        acc_q = sb("acc_q", [P, 2, 4, P])
        gT = sb("gT", [P, CHUNKS, COLS])
        st = sb("st", [P, 3, P])
        mean = sb("mean", [P, 2, P])
        rstd = sb("rstd", [P, 3, P])
        nt = sb("nt", [P, 4, P])
        t_tok = sb("t_tok", [P, 2, SPC, CH])
        tT = sb("tT", [P, 2, COLS])
        u = sb("u", [P, 2, COLS])
        x1T = sb("x1T", [P, 3, COLS])
        x1_sum = sb("x1_sum", [P, CHUNKS, BLK])
        rsum = sb("rsum", [P, CHUNKS, BLK])
        sig1 = sb("sig1", [P, 2, COLS])
        o_a = sb("o_a", [P, 2, COLS])
        oT = sb("oT", [P, 2, COLS])
        y = lr[:, 0:CH, :].rearrange("p f s -> p (f s)").rearrange("p (s c) -> p s c", c=CH)
        yn = lr[:, CH:2 * CH, :].rearrange("p f s -> p (f s)").rearrange("p (s c) -> p s c", c=CH)

        bank = ctx.enter_context(nc.psum_tensor("bank", [P, 8, COLS], fp32))

        def vec(name):
            i = len(MATS) * CH + VECS.index(name)
            return w_rep[:, i:i + 1]

        def mat(name):
            i = MATS.index(name) * CH
            return w_rep[:, i:i + CH]

        x_in = [sem(f"x_in{c}") for c in range(CHUNKS)]
        w_in, r_in, x_out = sem("w_in"), sem("r_in"), sem("x_out")
        zeroed, consts, blks, dvw, wstep = sem("zeroed"), sem("consts"), sem("blks"), sem("dvw"), sem("wstep")
        ctr_ready, oscaled, wprod, out0_ready = sem("ctr_ready"), sem("oscaled"), sem("wprod"), sem("out0_ready")
        mean1, centred1, squared1, xn_ready = sem("mean1"), sem("centred1"), sem("squared1"), sem("xn_ready")
        step = sem("step")
        xnT_ps, xnT_ready = sem("xnT_ps"), sem("xnT_ready")
        lr_ps, lr_sig, lr_ready = sem("lr_ps"), sem("lr_sig"), sem("lr_ready")
        tri_ps, p_ready, psq_ready = sem("tri_ps"), sem("p_ready"), sem("psq_ready")
        accq_pool, rstd2_ready = sem("accq_pool"), sem("rstd2_ready")
        pool_step = sem("pool_step")
        g_ps, g_ready = sem("g_ps"), sem("g_ready")
        t_ready, tT_ps, tT_ready = sem("t_ready"), sem("tT_ps"), sem("tT_ready")
        q_ps, xT_ps, u_ready, x1_ready = sem("q_ps"), sem("xT_ps"), sem("u_ready"), sem("x1_ready")
        rs_ps, rs_ready, l_ps, g1_ps, sig1_ready = (
            sem("rs_ps"), sem("rs_ready"), sem("l_ps"), sem("g1_ps"), sem("sig1_ready"))
        oa_ready, oT_ready = sem("oa_ready"), sem("oT_ready")
        y_ps, y_ready, ysq_ready, yn_ready = sem("y_ps"), sem("y_ready"), sem("ysq_ready"), sem("yn_ready")
        scaled, final = sem("scaled"), sem("final")

        TT, Q, XT, L, G, RS, Y = 0, 1, 2, 3, 4, 5, 6

        block = ctx.enter_context(nc.Block())

        @block.sync
        def _(sp):
            for c in range(CHUNKS):
                sp.dma_start(x_tok[:, c * SPC:(c + 1) * SPC, :],
                             x_tok_dram[:, c * SPC:(c + 1) * SPC, :]).then_inc(x_in[c], 16)
            for c in range(CHUNKS):
                sp.wait_ge(final, c + 1)
                sp.dma_start(out_tok_dram[:, c * SPC:(c + 1) * SPC, :],
                             sq[:, c * SPC:(c + 1) * SPC, :]).then_inc(x_out, 16)
            sp.wait_ge(x_out, 16 * CHUNKS)

        @block.gpsimd
        def _(pool):
            nc.gpsimd.memset(mask[:], 0.0).then_inc(zeroed, 1)
            nc.gpsimd.memset(ident[:], 0.0).then_inc(zeroed, 1)
            nc.gpsimd.memset(ones_rows[:], 0.0).then_inc(zeroed, 1)
            pool.wait_ge(zeroed, 3)
            nc.gpsimd.affine_select(out=ident[:], in_=ident[:], compare_op=ALU.not_equal, fill=1.0,
                                    base=0, pattern=[[-1, P]], channel_multiplier=1).then_inc(consts, 1)
            for g in range(GRP):
                pool.wait_ge(consts, 1 + g)
                nc.gpsimd.memset(mask[g * CH:(g + 1) * CH, g, :], 1.0).then_inc(consts, 1)
            for i in range(3):
                pool.wait_ge(consts, 5 + i)
                nc.gpsimd.memset(ones_rows[i * CH:i * CH + 1, :], 1.0).then_inc(consts, 1)
            pool.wait_ge(consts, 8)
            nc.gpsimd.memset(bo_rows[3 * CH:P], 0.0).then_inc(consts, 1)

            def center(b):
                lo, hi = LN1[b][0] * SPC, LN1[b][1] * SPC
                pool.wait_ge(mean1, b + 1)
                nc.gpsimd.tensor_tensor(xc[:, lo:hi, :], x_tok[:, lo:hi, :],
                                        mean[:, 0:1, lo:hi].rearrange("p a s -> p s a").to_broadcast([P, hi - lo, CH]),
                                        ALU.subtract).then_inc(centred1, 1)

            def block_diagonal(dst, src):
                nc.gpsimd.tensor_tensor(dst.rearrange("p (g c) -> p g c", g=GRP),
                                        src.rearrange("p (a c) -> p a c", a=1).to_broadcast([P, GRP, CH]),
                                        mask[:], ALU.mult).then_inc(blks, 1)

            pool.wait_ge(consts, 9)
            pool.wait_ge(w_in, 16)
            center(0)
            center(1)
            block_diagonal(out0_raw_blk[:], mat("out0"))
            center(2)
            block_diagonal(gate0_blk[:], mat("gate0"))
            nc.gpsimd.tensor_tensor(leq[:], mat("wleft"), mat("weq"), ALU.add).then_inc(pool_step, 1)
            nc.gpsimd.tensor_tensor(leq_bias[:], vec("b_left"), vec("b_eq"), ALU.add).then_inc(pool_step, 1)
            nc.gpsimd.tensor_scalar(right_bias[:], vec("b_right"), float(P), None, ALU.mult).then_inc(pool_step, 1)
            pool.wait_ge(pool_step, 3)
            block_diagonal(leq_blk[:], leq[:])
            block_diagonal(gate1_blk[:], mat("wgate"))
            block_diagonal(right_blk[:], mat("wright"))
            pool.wait_ge(dvw, 1)
            block_diagonal(wout_blk[:], wout_c[:])
            center(3)
            center(4)

            for b in range(1, 4):
                pool.wait_ge(psq_ready, b + 1)
                if b > 1:
                    pool.wait_ge(pool_step, 3 + b - 1)
                prev = p_sq[:, 0:4, :] if b == 1 else acc_q[:, 0]
                nc.gpsimd.tensor_tensor(acc_q[:, 0], prev, p_sq[:, 4 * b:4 * b + 4, :],
                                        ALU.add).then_inc(pool_step if b < 3 else accq_pool, 1)

            def normalise2(c):
                s = slice(c * SPC, (c + 1) * SPC)
                pool.wait_ge(rstd2_ready, 1)
                if c >= 2:
                    pool.wait_ge(tT_ps, c - 1)
                nc.gpsimd.tensor_tensor(t_tok[:, c % 2], p_sb[:, :, s].rearrange("p e s -> p s e"),
                                        rstd[:, 1:2, s].rearrange("p a s -> p s a").to_broadcast([P, SPC, CH]),
                                        ALU.mult).then_inc(t_ready, 1)

            def times_right(c):
                pool.wait_ge(oa_ready, c + 1)
                pool.wait_ge(rs_ready, c + 1)
                if c >= 2:
                    pool.wait_ge(y_ps, c - 1)
                nc.gpsimd.tensor_tensor(oT[:, c % 2].rearrange("p (b k) -> p b k", b=BLK),
                                        o_a[:, c % 2].rearrange("p (b k) -> p b k", b=BLK),
                                        rsum[:, c:c + 1, :].rearrange("p a b -> p b a").to_broadcast([P, BLK, P]),
                                        ALU.mult).then_inc(oT_ready, 1)

            def affine3(b):
                for c in range(*LN3[b]):
                    s = slice(c * SPC, (c + 1) * SPC)
                    pool.wait_ge(yn_ready, b + 1)
                    nc.gpsimd.tensor_tensor(yn[:, s, :], yn[:, s, :], row_rep[:, 0:1, :].to_broadcast([P, SPC, CH]),
                                            ALU.mult).then_inc(scaled, 1)
                    pool.wait_ge(scaled, c + 1)
                    nc.gpsimd.tensor_tensor(sq[:, s, :], yn[:, s, :], row_rep[:, 1:2, :].to_broadcast([P, SPC, CH]),
                                            ALU.add).then_inc(final, 1)

            pool.wait_ge(r_in, 16)
            for i in range(CHUNKS + 6):
                if i < CHUNKS:
                    normalise2(i)
                if 0 <= i - 2 < CHUNKS:
                    times_right(i - 2)
                for b, (lo, hi) in enumerate(LN3):
                    if hi - 1 == i - 4:
                        affine3(b)

        @block.scalar
        def _(act):
            act.dma_start(w_rep[:], weights.rearrange("(a p) n -> a p n", a=1).to_broadcast([GRP, CH, n_w])
                          ).then_inc(w_in, 16)
            act.dma_start(row_rep[:], rows.rearrange("(a v) c -> a v c", a=1).to_broadcast([P, len(ROWS), CH])
                          ).then_inc(r_in, 16)

            def square1(b):
                lo, hi = LN1[b][0] * SPC, LN1[b][1] * SPC
                act.wait_ge(centred1, b + 1)
                nc.scalar.activation(sq[:, lo:hi, :], xc[:, lo:hi, :], ACT.Square).then_inc(squared1, 1)

            def affine1(c):
                act.wait_ge(xnT_ps, c + 1)
                nc.scalar.activation(xnT[:, c], bank[:, c % 2], ACT.Identity, bias=vec("ln1_b"),
                                     scale=vec("ln1_w")).then_inc(xnT_ready, 1)

            def sigmoid_lr(c):
                for h in range(2):
                    j = 2 * c + h
                    act.wait_ge(lr_ps, j + 1)
                    if j >= 3:
                        act.wait_ge(lr_ready, j - 2)
                    lo = 2 + 2 * (j % 3)
                    src = bank[:, lo:lo + 2].rearrange("p b (s f) -> p (b s) f", f=4 * CH)
                    nc.scalar.activation(sig_lr[:, j % 3].rearrange("p (s f) -> p s f", f=2 * CH),
                                         src[:, :, 0:2 * CH], ACT.Sigmoid).then_inc(lr_sig, 1)

            act.wait_ge(w_in, 16)
            square1(0)
            square1(1)
            affine1(0)
            square1(2)
            affine1(1)
            for c in range(CHUNKS):
                sigmoid_lr(c)
                if c in (1, 3):
                    square1(3 + c // 2)
                if c + 2 < CHUNKS:
                    affine1(c + 2)

            for b in range(8):
                act.wait_ge(tri_ps, b + 1)
                src = bank[:, b].rearrange("p (e s) -> p e s", e=4)
                nc.scalar.activation(p_sb[:, 4 * b:4 * b + 4, :], src, ACT.Copy).then_inc(p_ready, 1)
                nc.scalar.activation(p_sq[:, 4 * b:4 * b + 4, :], src, ACT.Square).then_inc(psq_ready, 1)
            for c in range(CHUNKS):
                act.wait_ge(g_ps, c + 1)
                nc.scalar.activation(gT[:, c], bank[:, c], ACT.Sigmoid).then_inc(g_ready, 1)

            def evacuate_tT(c):
                act.wait_ge(tT_ps, c + 1)
                if c >= 2:
                    act.wait_ge(q_ps, c - 1)
                nc.scalar.activation(tT[:, c % 2], bank[:, TT], ACT.Copy).then_inc(tT_ready, 1)

            def right_and_gate(c):
                act.wait_ge(rs_ps, c + 1)
                nc.scalar.activation(rsum[:, c], bank[:, RS, 0:BLK], ACT.Identity,
                                     bias=right_bias[:]).then_inc(rs_ready, 1)
                act.wait_ge(g1_ps, c + 1)
                if c >= 2:
                    act.wait_ge(oa_ready, c - 1)
                nc.scalar.activation(sig1[:, c % 2], bank[:, G], ACT.Sigmoid, bias=vec("b_gate")
                                     ).then_inc(sig1_ready, 1)

            def evacuate_y(c):
                s = slice(c * SPC, (c + 1) * SPC)
                src = bank[:, Y + c % 2].rearrange("p (s c) -> p s c", c=CH)
                act.wait_ge(y_ps, c + 1)
                nc.scalar.activation(sq[:, s, :], src, ACT.Square).then_inc(ysq_ready, 1)
                nc.scalar.activation(y[:, s, :], src, ACT.Copy).then_inc(y_ready, 1)

            for i in range(CHUNKS + 3):
                if i < CHUNKS:
                    evacuate_tT(i)
                if 0 <= i - 2 < CHUNKS:
                    right_and_gate(i - 2)
                if 0 <= i - 3 < CHUNKS:
                    evacuate_y(i - 3)

        @block.vector
        def _(dve):
            steps = [0]

            def link(instruction):
                steps[0] += 1
                instruction.then_inc(step, 1)
                dve.wait_ge(step, steps[0])

            def rsqrt(i, lo, hi, done):
                v, r = st[:, i, lo:hi], rstd[:, i, lo:hi]
                bits, half, a, e = (nt[:, j, 0:hi - lo] for j in range(4))
                link(nc.vector.tensor_scalar(bits.bitcast(i32), v.bitcast(i32), 1, None, ALU.logical_shift_right))
                link(nc.vector.tensor_scalar(r.bitcast(i32), bits.bitcast(i32), -1.0, float(RSQRT_MAGIC),
                                             ALU.mult, ALU.add))
                link(nc.vector.tensor_scalar(half, v, -0.5, None, ALU.mult))
                for n in range(3):
                    link(nc.vector.tensor_tensor(a, r, r, ALU.mult))
                    link(nc.vector.tensor_tensor(e, a, half, ALU.mult))
                    last = nc.vector.scalar_tensor_tensor(out=r, in0=e, scalar=1.5, in1=r, op0=ALU.add, op1=ALU.mult)
                    if n < 2:
                        link(last)
                last.then_inc(done, 1)

            def mean_of(b):
                lo, hi = LN1[b][0] * SPC, LN1[b][1] * SPC
                for c in range(*LN1[b]):
                    dve.wait_ge(x_in[c], 16)
                link(nc.vector.tensor_reduce(mean[:, 1, lo:hi], x_tok[:, lo:hi, :], AX.X, ALU.add))
                nc.vector.tensor_scalar(mean[:, 0, lo:hi], mean[:, 1, lo:hi], 1.0 / CH, None,
                                        ALU.mult).then_inc(mean1, 1)

            rstd1 = sem("rstd1")

            def normalise1(b):
                lo, hi = LN1[b][0] * SPC, LN1[b][1] * SPC
                dve.wait_ge(squared1, b + 1)
                link(nc.vector.tensor_reduce(nt[:, 0, 0:hi - lo], sq[:, lo:hi, :], AX.X, ALU.add))
                link(nc.vector.tensor_scalar(st[:, 0, lo:hi], nt[:, 0, 0:hi - lo], 1.0 / CH, EPS, ALU.mult, ALU.add))
                rsqrt(0, lo, hi, rstd1)
                dve.wait_ge(rstd1, b + 1)
                nc.vector.tensor_tensor(xc[:, lo:hi, :], xc[:, lo:hi, :],
                                        rstd[:, 0:1, lo:hi].rearrange("p a s -> p s a").to_broadcast([P, hi - lo, CH]),
                                        ALU.mult).then_inc(xn_ready, 1)

            def multiply_lr(c):
                for h in range(2):
                    j = 2 * c + h
                    s = slice(c * SPC + h * SPC // 2, c * SPC + (h + 1) * SPC // 2)
                    lo = 2 + 2 * (j % 3)
                    src = bank[:, lo:lo + 2].rearrange("p b (s f) -> p (b s) f", f=4 * CH)
                    dve.wait_ge(lr_sig, j + 1)
                    nc.vector.tensor_tensor(lr[:, :, s].rearrange("p f s -> p s f"), src[:, :, 2 * CH:4 * CH],
                                            sig_lr[:, j % 3].rearrange("p (s f) -> p s f", f=2 * CH),
                                            ALU.mult).then_inc(lr_ready, 1)

            dve.wait_ge(w_in, 16)
            dve.wait_ge(consts, 5)
            nc.vector.tensor_tensor(
                lr_blk[:].rearrange("p g m c -> p g m c"),
                w_rep[:, 0:4 * CH].rearrange("p (a m c) -> p a m c", a=1, m=4).to_broadcast([P, GRP, 4, CH]),
                mask[:].rearrange("p g (a c) -> p g a c", a=1).to_broadcast([P, GRP, 4, CH]),
                ALU.mult).then_inc(ctr_ready, 1)
            mean_of(0)
            mean_of(1)
            nc.vector.scalar_tensor_tensor(out=center_blk[:], in0=mask[:].rearrange("p g c -> p (g c)"),
                                           scalar=-1.0 / CH, in1=ident[:], op0=ALU.mult,
                                           op1=ALU.add).then_inc(ctr_ready, 1)
            nc.vector.tensor_scalar(out0_scaled[:], mat("out0"), vec("ln2_w"), None, ALU.mult).then_inc(oscaled, 1)
            normalise1(0)
            mean_of(2)
            normalise1(1)
            link(nc.vector.tensor_reduce(wout_mean[:], mat("wout"), AX.X, ALU.add))
            link(nc.vector.tensor_scalar(wout_mean[:], wout_mean[:], 1.0 / CH, None, ALU.mult))
            nc.vector.tensor_scalar(wout_c[:], mat("wout"), wout_mean[:], None, ALU.subtract).then_inc(dvw, 1)
            for c in range(CHUNKS):
                if c % 2 == 0 and c < 6:
                    normalise1(2 + c // 2)
                if c in (1, 3):
                    mean_of(3 + c // 2)
                multiply_lr(c)
                if c == 0:
                    dve.wait_ge(wprod, 1)
                    nc.vector.tensor_tensor(out0_blk[:].rearrange("p (g c) -> p g c", g=GRP),
                                            bank[:, 7, 0:CH].rearrange("p (a c) -> p a c", a=1).to_broadcast([P, GRP, CH]),
                                            mask[:], ALU.mult).then_inc(out0_ready, 1)
                    nc.vector.tensor_copy(q_bias[:], bank[:, 7, CH:CH + 1]).then_inc(out0_ready, 1)
                if c == 6:
                    dve.wait_ge(r_in, 16)
                    link(nc.vector.tensor_reduce(bo_mean[:], row_rep[:, 2, :], AX.X, ALU.add))
                    link(nc.vector.tensor_scalar(bo_mean[:], bo_mean[:], 1.0 / CH, None, ALU.mult))
                    link(nc.vector.tensor_scalar(bo_c[:, 0], row_rep[:, 2, :], bo_mean[:], None, ALU.subtract))
                    for i in range(3):
                        link(nc.vector.tensor_copy(bo_part[:, i], bo_c[:, i]))
                        if i < 2:
                            link(nc.vector.tensor_tensor(bo_c[:, i + 1], bo_c[:, i], bo_part[:, i], ALU.subtract))
                    for i in range(3):
                        g = slice(i * CH, (i + 1) * CH)
                        nc.vector.tensor_copy(bo_rows[g], bo_part[g, i:i + 1, :].to_broadcast([CH, SPC, CH])
                                              ).then_inc(dvw, 1)

            for b in range(1, 8):
                dve.wait_ge(p_ready, b + 1)
                prev = p_sb[:, 0:4, :] if b == 1 else acc_p[:]
                link(nc.vector.tensor_tensor(acc_p[:], prev, p_sb[:, 4 * b:4 * b + 4, :], ALU.add))
                if b > 4:
                    dve.wait_ge(psq_ready, b + 1)
                    prev = p_sq[:, 16:20, :] if b == 5 else acc_q[:, 1]
                    link(nc.vector.tensor_tensor(acc_q[:, 1], prev, p_sq[:, 4 * b:4 * b + 4, :], ALU.add))
            link(nc.vector.tensor_tensor(acc_p[:, 0:2], acc_p[:, 0:2], acc_p[:, 2:4], ALU.add))
            link(nc.vector.tensor_tensor(acc_p[:, 0], acc_p[:, 0], acc_p[:, 1], ALU.add))
            dve.wait_ge(accq_pool, 1)
            link(nc.vector.tensor_tensor(acc_q[:, 0], acc_q[:, 0], acc_q[:, 1], ALU.add))
            link(nc.vector.tensor_tensor(acc_q[:, 0, 0:2], acc_q[:, 0, 0:2], acc_q[:, 0, 2:4], ALU.add))
            link(nc.vector.tensor_tensor(acc_q[:, 0, 0], acc_q[:, 0, 0], acc_q[:, 0, 1], ALU.add))
            link(nc.vector.tensor_scalar(acc_p[:, 0], acc_p[:, 0], 1.0 / CH, None, ALU.mult))
            link(nc.vector.tensor_tensor(acc_p[:, 1], acc_p[:, 0], acc_p[:, 0], ALU.mult))
            link(nc.vector.tensor_scalar(acc_q[:, 0, 0], acc_q[:, 0, 0], 1.0 / CH, EPS, ALU.mult, ALU.add))
            link(nc.vector.tensor_tensor(st[:, 1], acc_q[:, 0, 0], acc_p[:, 1], ALU.subtract))
            rsqrt(1, 0, P, rstd2_ready)

            def residual0(c):
                dve.wait_ge(q_ps, c + 1)
                dve.wait_ge(g_ready, c + 1)
                link(nc.vector.scalar_tensor_tensor(out=u[:, c % 2], in0=bank[:, Q], scalar=q_bias[:], in1=gT[:, c],
                                                    op0=ALU.add, op1=ALU.mult))
                dve.wait_ge(xT_ps, c + 1)
                if c >= 3:
                    dve.wait_ge(y_ps, c - 2)
                for j in range(BLK):
                    b = slice(j * P, (j + 1) * P)
                    nc.vector.scalar_tensor_tensor(out=x1T[:, c % 3, b], in0=bank[:, XT, b], scalar=0.0,
                                                   in1=u[:, c % 2, b], op0=ALU.add, op1=ALU.add,
                                                   accum_out=x1_sum[:, c, j:j + 1]).then_inc(x1_ready, 1)

            def gated1(c):
                dve.wait_ge(l_ps, c + 1)
                dve.wait_ge(sig1_ready, c + 1)
                if c >= 2:
                    dve.wait_ge(oT_ready, c - 1)
                nc.vector.scalar_tensor_tensor(out=o_a[:, c % 2], in0=bank[:, L], scalar=leq_bias[:],
                                               in1=sig1[:, c % 2], op0=ALU.add, op1=ALU.mult).then_inc(oa_ready, 1)

            rstd3 = sem("rstd3")

            def normalise3(b):
                lo, hi = LN3[b][0] * SPC, LN3[b][1] * SPC
                dve.wait_ge(y_ready, LN3[b][1])
                dve.wait_ge(ysq_ready, LN3[b][1])
                link(nc.vector.tensor_reduce(nt[:, 0, 0:hi - lo], sq[:, lo:hi, :], AX.X, ALU.add))
                link(nc.vector.tensor_scalar(st[:, 2, lo:hi], nt[:, 0, 0:hi - lo], 1.0 / CH, EPS, ALU.mult, ALU.add))
                rsqrt(2, lo, hi, rstd3)
                dve.wait_ge(rstd3, b + 1)
                nc.vector.tensor_tensor(yn[:, lo:hi, :], y[:, lo:hi, :],
                                        rstd[:, 2:3, lo:hi].rearrange("p a s -> p s a").to_broadcast([P, hi - lo, CH]),
                                        ALU.mult).then_inc(yn_ready, 1)

            dve.wait_ge(out0_ready, 2)
            for i in range(CHUNKS + 4):
                if 0 <= i - 1 < CHUNKS:
                    residual0(i - 1)
                if 0 <= i - 2 < CHUNKS:
                    gated1(i - 2)
                for b, (lo, hi) in enumerate(LN3):
                    if hi - 1 == i - 4:
                        normalise3(b)

        @block.tensor
        def _(pe):
            def transpose_xn(c):
                b = next(n for n, (lo, hi) in enumerate(LN1) if lo <= c < hi)
                pe.wait_ge(xn_ready, b + 1)
                if c >= 2:
                    pe.wait_ge(xnT_ready, c - 1)
                for j in range(BLK):
                    s = c * SPC + j * GRP
                    last = nc.tensor.transpose(bank[:, c % 2, j * P:(j + 1) * P],
                                               xc[:, s:s + GRP, :].rearrange("p s c -> p (s c)"), ident[:])
                last.then_inc(xnT_ps, 1)

            def project_lr(c):
                pe.wait_ge(xnT_ready, c + 1)
                for h in range(2):
                    j = 2 * c + h
                    if j >= 3:
                        pe.wait_ge(lr_ready, j - 2)
                    for n in range(2):
                        k = 2 * h + n
                        last = nc.tensor.matmul(bank[:, 2 + 2 * (j % 3) + n], xnT[:, c, k * P:(k + 1) * P],
                                                lr_blk[:].rearrange("p g m c -> p (g m c)"), start=True, stop=True)
                    last.then_inc(lr_ps, 1)

            pe.wait_ge(consts, 5)
            transpose_xn(0)
            pe.wait_ge(ctr_ready, 2)
            pe.wait_ge(oscaled, 1)
            nc.tensor.matmul(bank[:, 7, 0:CH], center_blk[:], out0_scaled[:], start=True, stop=True)
            pe.wait_ge(blks, 1)
            nc.tensor.matmul(bank[:, 7, CH:CH + 1], out0_raw_blk[:], vec("ln2_b"), start=True, stop=True
                             ).then_inc(wprod, 1)
            transpose_xn(1)
            for c in range(CHUNKS):
                if c == 1:
                    pe.wait_ge(out0_ready, 2)
                project_lr(c)
                if c + 2 < CHUNKS:
                    transpose_xn(c + 2)

            pe.wait_ge(lr_ready, 2 * CHUNKS)
            pe.wait_ge(xnT_ready, CHUNKS)
            for e in range(CH):
                last = nc.tensor.matmul(bank[:, e // 4, (e % 4) * P:(e % 4 + 1) * P], lr[:, e, :], lr[:, CH + e, :],
                                        start=True, stop=True)
                if e % 4 == 3:
                    last.then_inc(tri_ps, 1)

            pe.wait_ge(blks, 2)
            for c in range(CHUNKS):
                pe.wait_ge(psq_ready, c + 1)
                nc.tensor.matmul(bank[:, c], gate0_blk[:], xnT[:, c], start=True, stop=True).then_inc(g_ps, 1)

            def transpose_t(c):
                pe.wait_ge(t_ready, c + 1)
                pe.wait_ge(tT_ready, c) if c else pe.wait_ge(g_ready, TT + 1)
                for j in range(BLK):
                    last = nc.tensor.transpose(bank[:, TT, j * P:(j + 1) * P],
                                               t_tok[:, c % 2, j * GRP:(j + 1) * GRP, :].rearrange("p s c -> p (s c)"),
                                               ident[:])
                last.then_inc(tT_ps, 1)

            def project_q(c):
                pe.wait_ge(tT_ready, c + 1)
                if c:
                    pe.wait_ge(x1_ready, BLK * c)
                else:
                    pe.wait_ge(g_ready, XT + 1)
                nc.tensor.matmul(bank[:, Q], out0_blk[:], tT[:, c % 2], start=True, stop=True).then_inc(q_ps, 1)
                for j in range(BLK):
                    s = c * SPC + j * GRP
                    last = nc.tensor.transpose(bank[:, XT, j * P:(j + 1) * P],
                                               x_tok[:, s:s + GRP, :].rearrange("p s c -> p (s c)"), ident[:])
                last.then_inc(xT_ps, 1)

            def project_1(c):
                pe.wait_ge(x1_ready, BLK * (c + 1))
                pe.wait_ge(rs_ready, c) if c else pe.wait_ge(g_ready, RS + 1)
                nc.tensor.matmul(bank[:, RS, 0:BLK], right_blk[:], x1_sum[:, c], start=True, stop=True
                                 ).then_inc(rs_ps, 1)
                if c:
                    pe.wait_ge(sig1_ready, c)
                nc.tensor.matmul(bank[:, G], gate1_blk[:], x1T[:, c % 3], start=True, stop=True).then_inc(g1_ps, 1)
                if c:
                    pe.wait_ge(oa_ready, c)
                nc.tensor.matmul(bank[:, L], leq_blk[:], x1T[:, c % 3], start=True, stop=True).then_inc(l_ps, 1)

            def project_y(c):
                b = Y + c % 2
                if c >= 2:
                    pe.wait_ge(y_ready, c - 1)
                elif c == 0:
                    pe.wait_ge(g_ready, CHUNKS)
                nc.tensor.matmul(bank[:, b], ones_rows[:], bo_rows[:].rearrange("p s c -> p (s c)"),
                                 start=True, stop=False, skip_group_check=True)
                for j in range(BLK):
                    k = slice(j * P, (j + 1) * P)
                    nc.tensor.matmul(bank[:, b, k], x1T[:, c % 3, k], center_blk[:], start=False, stop=False,
                                     skip_group_check=True)
                pe.wait_ge(oT_ready, c + 1)
                for j in range(BLK):
                    k = slice(j * P, (j + 1) * P)
                    last = nc.tensor.matmul(bank[:, b, k], oT[:, c % 2, k], wout_blk[:], start=False,
                                            stop=j == BLK - 1, skip_group_check=True)
                last.then_inc(y_ps, 1)

            pe.wait_ge(blks, 6)
            pe.wait_ge(dvw, 4)
            pe.wait_ge(consts, 9)
            for i in range(CHUNKS + 3):
                if i < CHUNKS:
                    transpose_t(i)
                if 0 <= i - 1 < CHUNKS:
                    project_q(i - 1)
                if 0 <= i - 2 < CHUNKS:
                    project_1(i - 2)
                if 0 <= i - 3 < CHUNKS:
                    project_y(i - 3)


def kernel(**inputs):
    import numpy as _np
    import concourse.bacc as _bacc
    from concourse import mybir as _mybir
    from concourse.bass_utils import run_bass_kernel_spmd as _run

    a = {k: _np.asarray(v) for k, v in inputs.items()}
    mats = [a["L0_conv_" + n] for n in ("left1", "right1", "left2", "right2", "gate", "out_w")]
    mats += [a["L1_conv_W_" + n] for n in ("left", "eq", "gate", "right", "out")]
    vecs = [a["L0_conv_" + n] for n in ("ln1_w", "ln1_b", "ln2_w", "ln2_b")]
    vecs += [a["L1_conv_b_" + n] for n in ("left", "eq", "right", "gate")]
    rows = [a["L1_conv_ln_scale"], a["L1_conv_ln_bias"], a["L1_conv_b_out"]]
    arrays = {
        "in_x": _np.ascontiguousarray(a["x"]),
        "in_weights": _np.concatenate(mats + [v[:, None] for v in vecs], axis=1),
        "in_rows": _np.stack(rows),
    }
    nc = _bacc.Bacc("TRN2", target_bir_lowering=False, num_devices=1)
    args = [nc.dram_tensor(n, v.shape, _mybir.dt.from_np(v.dtype), kind="ExternalInput").ap()
            for n, v in arrays.items()]
    args.append(nc.dram_tensor("out", a["x"].shape, _mybir.dt.float32, kind="ExternalOutput").ap())
    pair_layers(nc, *args)
    r = _run(nc, [arrays], core_ids=[0])
    return r.results[0]["out"]
```

```python
import concourse.bass as bass
from concourse import mybir
from contextlib import ExitStack

P = 128
CH = 32
GRP = P // CH
CHUNKS = 8
SPC = P // CHUNKS
COLS = SPC * CH
BLK = COLS // P
EPS = 1e-5

MATS = ["left1", "right1", "left2", "right2", "gate0", "out0", "wleft", "weq", "wgate", "wright", "wout"]
VECS = ["ln1_w", "ln1_b", "ln2_w", "ln2_b", "b_left", "b_eq", "b_right", "b_gate"]
ROWS = ["ln_scale", "ln_bias", "b_out"]

SUMS1 = [(0, 1), (1, 2), (2, 3), (3, 4), (4, 6), (6, 8)]
ROOTS1 = [(0, 1), (1, 2), (2, 3), (3, 4), (4, 8)]
OWN_CENTRE = 2
ROOTS3 = [(0, 4), (4, 6), (6, 7), (7, 8)]
FINAL_AT = {8: [0, 1], 9: [2, 3]}
POOL_SQ = 5


def pair_layers(nc, x, weights, rows, out):
    fp32, bf16 = mybir.dt.float32, mybir.dt.bfloat16
    ALU, ACT, AX = mybir.AluOpType, mybir.ActivationFunctionType, mybir.AxisListType

    x_tok_dram = x[0].rearrange("s r c -> r s c")
    out_tok_dram = out[0].rearrange("s r c -> r s c")
    n_w = weights.shape[1]

    with ExitStack() as ctx:
        def sb(name, shape, dt=fp32):
            return ctx.enter_context(nc.sbuf_tensor(name, shape, dt))

        def sem(name):
            return ctx.enter_context(nc.semaphore(name))

        w_rep = sb("w_rep", [P, n_w])
        row_rep = sb("row_rep", [P, len(ROWS), CH])
        mask = sb("mask", [P, GRP, CH])
        ident = sb("ident", [P, P])
        center_blk = sb("center_blk", [P, P])
        lr_blk = sb("lr_blk", [P, GRP, 4, CH])
        gate0_blk = sb("gate0_blk", [P, P])
        out0_raw_blk = sb("out0_raw_blk", [P, P])
        out0_scaled = sb("out0_scaled", [P, CH])
        out0_blk = sb("out0_blk", [P, P])
        q_bias = sb("q_bias", [P, 1])
        leq = sb("leq", [P, CH])
        leq_blk = sb("leq_blk", [P, P])
        leq_bias = sb("leq_bias", [P, 1])
        gate1_blk = sb("gate1_blk", [P, P])
        right_blk = sb("right_blk", [P, P])
        right_bias = sb("right_bias", [P, 1])
        wout_mean = sb("wout_mean", [P, 1])
        wout_c = sb("wout_c", [P, CH])
        wout_blk = sb("wout_blk", [P, P])
        bo_mean = sb("bo_mean", [P, 1])
        bo_c = sb("bo_c", [P, 3, CH])
        bo_part = sb("bo_part", [P, 3, CH], bf16)
        bo_rows = sb("bo_rows", [P, SPC, CH], bf16)
        ones_rows = sb("ones_rows", [P, P], bf16)

        x_tok = sb("x_tok", [P, P, CH])
        xc = sb("xc", [P, P, CH])
        sq = sb("sq", [P, P, CH])
        xnT = sb("xnT", [P, CHUNKS, COLS])
        sig_lr = sb("sig_lr", [P, 3, 2 * COLS // 2])
        lr = sb("lr", [P, 2 * CH, P])
        p_sb = sb("p_sb", [P, CH, P])
        p_sq = sb("p_sq", [P, CH, P])
        acc_p = sb("acc_p", [P, 4, P])
        acc_q = sb("acc_q", [P, 2, 4, P])
        gT = sb("gT", [P, CHUNKS, COLS])
        st = sb("st", [P, 3, P])
        mean = sb("mean", [P, 2, P])
        std = sb("std", [P, 3, P])
        rstd = sb("rstd", [P, 3, P])
        eps = sb("eps", [P, 1])
        t_tok = sb("t_tok", [P, 2, SPC, CH])
        tT = sb("tT", [P, 2, COLS])
        u = sb("u", [P, 2, COLS])
        x1T = sb("x1T", [P, 3, COLS])
        x1_sum = sb("x1_sum", [P, CHUNKS, BLK])
        rsum = sb("rsum", [P, CHUNKS, BLK])
        sig1 = sb("sig1", [P, 2, COLS])
        o_a = sb("o_a", [P, 2, COLS])
        oT = sb("oT", [P, 2, COLS])
        y = lr[:, 0:CH, :].rearrange("p f s -> p (f s)").rearrange("p (s c) -> p s c", c=CH)
        yn = lr[:, CH:2 * CH, :].rearrange("p f s -> p (f s)").rearrange("p (s c) -> p s c", c=CH)

        bank = ctx.enter_context(nc.psum_tensor("bank", [P, 8, COLS], fp32))

        def vec(name):
            i = len(MATS) * CH + VECS.index(name)
            return w_rep[:, i:i + 1]

        def mat(name):
            i = MATS.index(name) * CH
            return w_rep[:, i:i + CH]

        x_in = [sem(f"x_in{c}") for c in range(CHUNKS)]
        w_in, r_in, x_out = sem("w_in"), sem("r_in"), sem("x_out")
        zeroed, consts, blks, dvw, wstep = sem("zeroed"), sem("consts"), sem("blks"), sem("dvw"), sem("wstep")
        ctr_ready, oscaled, wprod, out0_ready = sem("ctr_ready"), sem("oscaled"), sem("wprod"), sem("out0_ready")
        mean1, centred1_pool, centred1, squared1 = sem("mean1"), sem("centred1_pool"), sem("centred1"), sem("squared1")
        var1, root1, rstd1, xn_ready, xn_pool = sem("var1"), sem("root1"), sem("rstd1"), sem("xn_ready"), sem("xn_pool")
        step, eps_set, warm = sem("step"), sem("eps_set"), sem("warm")
        xnT_ps, xnT_ready = sem("xnT_ps"), sem("xnT_ready")
        lr_ps, lr_sig, lr_ready = sem("lr_ps"), sem("lr_sig"), sem("lr_ready")
        tri_ps, p_ready, psq_ready = sem("tri_ps"), sem("p_ready"), sem("psq_ready")
        accq_pool, var2, root2, rstd2 = sem("accq_pool"), sem("var2"), sem("root2"), sem("rstd2")
        pool_step = sem("pool_step")
        g_ps, g_ready = sem("g_ps"), sem("g_ready")
        t0_ready, t_ready, tT_ps, tT_ready = sem("t0_ready"), sem("t_ready"), sem("tT_ps"), sem("tT_ready")
        q_ps, xT_ps, u_ready, x1_ready = sem("q_ps"), sem("xT_ps"), sem("u_ready"), sem("x1_ready")
        rs_ps, rs_ready, l_ps, g1_ps, sig1_ready = (
            sem("rs_ps"), sem("rs_ready"), sem("l_ps"), sem("g1_ps"), sem("sig1_ready"))
        oa_ready, oT_ready = sem("oa_ready"), sem("oT_ready")
        y_ps, y_ready, ysq_ready, yn_ready = sem("y_ps"), sem("y_ready"), sem("ysq_ready"), sem("yn_ready")
        var3, root3, rstd3 = sem("var3"), sem("root3"), sem("rstd3")
        scaled, final = sem("scaled"), sem("final")

        TT, Q, XT, L, G, RS, Y = 0, 1, 2, 3, 4, 5, 6

        block = ctx.enter_context(nc.Block())

        @block.sync
        def _(sp):
            for c in range(CHUNKS):
                sp.dma_start(x_tok[:, c * SPC:(c + 1) * SPC, :],
                             x_tok_dram[:, c * SPC:(c + 1) * SPC, :]).then_inc(x_in[c], 16)
            for c in range(CHUNKS):
                sp.wait_ge(final, c + 1)
                sp.dma_start(out_tok_dram[:, c * SPC:(c + 1) * SPC, :],
                             sq[:, c * SPC:(c + 1) * SPC, :]).then_inc(x_out, 16)
            sp.wait_ge(x_out, 16 * CHUNKS)

        @block.gpsimd
        def _(pool):
            nc.gpsimd.memset(mask[:], 0.0).then_inc(zeroed, 1)
            nc.gpsimd.memset(ident[:], 0.0).then_inc(zeroed, 1)
            nc.gpsimd.memset(ones_rows[:], 0.0).then_inc(zeroed, 1)
            pool.wait_ge(zeroed, 3)
            nc.gpsimd.affine_select(out=ident[:], in_=ident[:], compare_op=ALU.not_equal, fill=1.0,
                                    base=0, pattern=[[-1, P]], channel_multiplier=1).then_inc(consts, 1)
            for g in range(GRP):
                pool.wait_ge(consts, 1 + g)
                nc.gpsimd.memset(mask[g * CH:(g + 1) * CH, g, :], 1.0).then_inc(consts, 1)
            for i in range(3):
                pool.wait_ge(consts, 5 + i)
                nc.gpsimd.memset(ones_rows[i * CH:i * CH + 1, :], 1.0).then_inc(consts, 1)
            pool.wait_ge(consts, 8)
            nc.gpsimd.memset(bo_rows[3 * CH:P], 0.0).then_inc(consts, 1)

            def center(b):
                lo, hi = SUMS1[b][0] * SPC, SUMS1[b][1] * SPC
                pool.wait_ge(mean1, b + 1 - OWN_CENTRE)
                nc.gpsimd.tensor_tensor(xc[:, lo:hi, :], x_tok[:, lo:hi, :],
                                        mean[:, 0:1, lo:hi].rearrange("p a s -> p s a").to_broadcast([P, hi - lo, CH]),
                                        ALU.subtract).then_inc(centred1_pool, 1)

            def normalise1(c):
                s = slice(c * SPC, (c + 1) * SPC)
                pool.wait_ge(rstd1, next(n for n, (lo, hi) in enumerate(ROOTS1) if lo <= c < hi) + 1)
                nc.gpsimd.tensor_tensor(xc[:, s, :], xc[:, s, :],
                                        rstd[:, 0:1, s].rearrange("p a s -> p s a").to_broadcast([P, SPC, CH]),
                                        ALU.mult).then_inc(xn_pool, 1)

            def block_diagonal(dst, src):
                nc.gpsimd.tensor_tensor(dst.rearrange("p (g c) -> p g c", g=GRP),
                                        src.rearrange("p (a c) -> p a c", a=1).to_broadcast([P, GRP, CH]),
                                        mask[:], ALU.mult).then_inc(blks, 1)

            pool.wait_ge(consts, 9)
            pool.wait_ge(w_in, 16)
            block_diagonal(out0_raw_blk[:], mat("out0"))
            center(2)
            block_diagonal(gate0_blk[:], mat("gate0"))
            center(3)
            normalise1(2)
            nc.gpsimd.tensor_tensor(leq[:], mat("wleft"), mat("weq"), ALU.add).then_inc(pool_step, 1)
            nc.gpsimd.tensor_tensor(leq_bias[:], vec("b_left"), vec("b_eq"), ALU.add).then_inc(pool_step, 1)
            nc.gpsimd.tensor_scalar(right_bias[:], vec("b_right"), float(P), None, ALU.mult).then_inc(pool_step, 1)
            center(4)
            normalise1(3)
            center(5)
            for c in range(4, CHUNKS):
                normalise1(c)
            pool.wait_ge(pool_step, 3)
            block_diagonal(leq_blk[:], leq[:])
            block_diagonal(gate1_blk[:], mat("wgate"))
            block_diagonal(right_blk[:], mat("wright"))
            pool.wait_ge(dvw, 1)
            block_diagonal(wout_blk[:], wout_c[:])

            for b in range(1, POOL_SQ):
                pool.wait_ge(psq_ready, b + 1)
                if b > 1:
                    pool.wait_ge(pool_step, 3 + b - 1)
                prev = p_sq[:, 0:4, :] if b == 1 else acc_q[:, 0]
                nc.gpsimd.tensor_tensor(acc_q[:, 0], prev, p_sq[:, 4 * b:4 * b + 4, :],
                                        ALU.add).then_inc(pool_step if b < POOL_SQ - 1 else accq_pool, 1)

            def normalise2(c):
                s = slice(c * SPC, (c + 1) * SPC)
                pool.wait_ge(rstd2, 1 if c < 2 else 2)
                if c >= 2:
                    pool.wait_ge(tT_ps, c - 1)
                nc.gpsimd.tensor_tensor(t_tok[:, c % 2], p_sb[:, :, s].rearrange("p e s -> p s e"),
                                        rstd[:, 1:2, s].rearrange("p a s -> p s a").to_broadcast([P, SPC, CH]),
                                        ALU.mult).then_inc(t_ready, 1)

            def times_right(c):
                pool.wait_ge(oa_ready, c + 1)
                pool.wait_ge(rs_ready, c + 1)
                if c >= 2:
                    pool.wait_ge(y_ps, c - 1)
                nc.gpsimd.tensor_tensor(oT[:, c % 2].rearrange("p (b k) -> p b k", b=BLK),
                                        o_a[:, c % 2].rearrange("p (b k) -> p b k", b=BLK),
                                        rsum[:, c:c + 1, :].rearrange("p a b -> p b a").to_broadcast([P, BLK, P]),
                                        ALU.mult).then_inc(oT_ready, 1)

            def bias3(c):
                s = slice(c * SPC, (c + 1) * SPC)
                pool.wait_ge(scaled, c + 1)
                nc.gpsimd.tensor_tensor(sq[:, s, :], yn[:, s, :], row_rep[:, 1:2, :].to_broadcast([P, SPC, CH]),
                                        ALU.add).then_inc(final, 1)

            pool.wait_ge(r_in, 16)
            normalise2(1)
            for i in range(CHUNKS + 2):
                if i >= 2:
                    times_right(i - 2)
                if i + 2 < CHUNKS:
                    normalise2(i + 2)
                for c in FINAL_AT.get(i, []):
                    bias3(c)
            for c in range(4, CHUNKS):
                bias3(c)

        @block.scalar
        def _(act):
            act.dma_start(w_rep[:], weights.rearrange("(a p) n -> a p n", a=1).to_broadcast([GRP, CH, n_w])
                          ).then_inc(w_in, 16)
            act.dma_start(row_rep[:], rows.rearrange("(a v) c -> a v c", a=1).to_broadcast([P, len(ROWS), CH])
                          ).then_inc(r_in, 16)

            def square1(b):
                lo, hi = SUMS1[b][0] * SPC, SUMS1[b][1] * SPC
                if b < OWN_CENTRE:
                    act.wait_ge(centred1, b + 1)
                else:
                    act.wait_ge(centred1_pool, b + 1 - OWN_CENTRE)
                nc.scalar.activation(sq[:, lo:hi, :], xc[:, lo:hi, :], ACT.Square).then_inc(squared1, 1)

            def root(layer, chunks, done):
                lo, hi = chunks[0] * SPC, chunks[1] * SPC
                nc.scalar.activation(std[:, layer, lo:hi], st[:, layer, lo:hi], ACT.Sqrt, scale=1.0 / CH,
                                     bias=eps[:]).then_inc(done, 1)

            def root1_of(b):
                act.wait_ge(var1, 6 if b == len(ROOTS1) - 1 else b + 1)
                root(0, ROOTS1[b], root1)

            def affine1(c):
                act.wait_ge(xnT_ps, c + 1)
                nc.scalar.activation(xnT[:, c], bank[:, c % 2], ACT.Identity, bias=vec("ln1_b"),
                                     scale=vec("ln1_w")).then_inc(xnT_ready, 1)

            def sigmoid_lr(c):
                for h in range(2):
                    j = 2 * c + h
                    act.wait_ge(lr_ps, j + 1)
                    if j >= 3:
                        act.wait_ge(lr_ready, j - 2)
                    lo = 2 + 2 * (j % 3)
                    src = bank[:, lo:lo + 2].rearrange("p b (s f) -> p (b s) f", f=4 * CH)
                    nc.scalar.activation(sig_lr[:, j % 3].rearrange("p (s f) -> p s f", f=2 * CH),
                                         src[:, :, 0:2 * CH], ACT.Sigmoid).then_inc(lr_sig, 1)

            act.wait_ge(eps_set, 1)
            nc.scalar.activation(std[:, 0, 0:1], eps[:], ACT.Sqrt).then_inc(warm, 1)
            act.wait_ge(warm, 1)
            square1(0)
            root1_of(0)
            square1(1)
            root1_of(1)
            act.wait_ge(w_in, 16)
            affine1(0)
            square1(2)
            root1_of(2)
            affine1(1)
            square1(3)
            root1_of(3)
            for c in range(CHUNKS):
                sigmoid_lr(c)
                if c in (0, 1):
                    square1(4 + c)
                if c + 2 < CHUNKS:
                    affine1(c + 2)
                if c == 1:
                    root1_of(4)

            for b in range(8):
                act.wait_ge(tri_ps, b + 1)
                src = bank[:, b].rearrange("p (e s) -> p e s", e=4)
                nc.scalar.activation(p_sb[:, 4 * b:4 * b + 4, :], src, ACT.Copy).then_inc(p_ready, 1)
                nc.scalar.activation(p_sq[:, 4 * b:4 * b + 4, :], src, ACT.Square).then_inc(psq_ready, 1)
            for c in range(CHUNKS):
                if c == 4:
                    act.wait_ge(var2, 1)
                    root(1, (0, CHUNKS), root2)
                act.wait_ge(g_ps, c + 1)
                nc.scalar.activation(gT[:, c], bank[:, c], ACT.Sigmoid).then_inc(g_ready, 1)

            def evacuate_tT(c):
                act.wait_ge(tT_ps, c + 1)
                if c >= 2:
                    act.wait_ge(q_ps, c - 1)
                nc.scalar.activation(tT[:, c % 2], bank[:, TT], ACT.Copy).then_inc(tT_ready, 1)

            def right_and_gate(c):
                act.wait_ge(rs_ps, c + 1)
                nc.scalar.activation(rsum[:, c], bank[:, RS, 0:BLK], ACT.Identity,
                                     bias=right_bias[:]).then_inc(rs_ready, 1)
                act.wait_ge(g1_ps, c + 1)
                if c >= 2:
                    act.wait_ge(oa_ready, c - 1)
                nc.scalar.activation(sig1[:, c % 2], bank[:, G], ACT.Sigmoid, bias=vec("b_gate")
                                     ).then_inc(sig1_ready, 1)

            def evacuate_y(c):
                s = slice(c * SPC, (c + 1) * SPC)
                src = bank[:, Y + c % 2].rearrange("p (s c) -> p s c", c=CH)
                act.wait_ge(y_ps, c + 1)
                nc.scalar.activation(sq[:, s, :], src, ACT.Square).then_inc(ysq_ready, 1)
                nc.scalar.activation(y[:, s, :], src, ACT.Copy).then_inc(y_ready, 1)

            def root3_of(b):
                act.wait_ge(var3, ROOTS3[b][1])
                root(2, ROOTS3[b], root3)

            for i in range(CHUNKS + 3):
                if i < CHUNKS:
                    evacuate_tT(i)
                if 0 <= i - 2 < CHUNKS:
                    right_and_gate(i - 2)
                if i == 7:
                    root3_of(0)
                if i == CHUNKS + 1:
                    root3_of(1)
                if 0 <= i - 3 < CHUNKS:
                    evacuate_y(i - 3)
            root3_of(2)
            root3_of(3)

        @block.vector
        def _(dve):
            steps = [0]

            def link(instruction):
                steps[0] += 1
                instruction.then_inc(step, 1)
                dve.wait_ge(step, steps[0])

            def mean_of(b):
                lo, hi = SUMS1[b][0] * SPC, SUMS1[b][1] * SPC
                for c in range(*SUMS1[b]):
                    dve.wait_ge(x_in[c], 16)
                link(nc.vector.tensor_reduce(mean[:, 1, lo:hi], x_tok[:, lo:hi, :], AX.X, ALU.add))
                if b < OWN_CENTRE:
                    sums = mean[:, 1:2, lo:hi].rearrange("p a s -> p s a").to_broadcast([P, hi - lo, CH])
                    nc.vector.scalar_tensor_tensor(out=xc[:, lo:hi, :], in0=sums, scalar=-1.0 / CH,
                                                   in1=x_tok[:, lo:hi, :], op0=ALU.mult, op1=ALU.add
                                                   ).then_inc(centred1, 1)
                else:
                    nc.vector.tensor_scalar(mean[:, 0, lo:hi], mean[:, 1, lo:hi], 1.0 / CH, None,
                                            ALU.mult).then_inc(mean1, 1)

            def variance1(b):
                lo, hi = SUMS1[b][0] * SPC, SUMS1[b][1] * SPC
                dve.wait_ge(squared1, b + 1)
                nc.vector.tensor_reduce(st[:, 0, lo:hi], sq[:, lo:hi, :], AX.X, ALU.add).then_inc(var1, 1)

            def inverse1(b):
                lo, hi = ROOTS1[b][0] * SPC, ROOTS1[b][1] * SPC
                dve.wait_ge(root1, b + 1)
                nc.vector.reciprocal(rstd[:, 0, lo:hi], std[:, 0, lo:hi]).then_inc(rstd1, 1)
                if b < OWN_CENTRE:
                    dve.wait_ge(rstd1, b + 1)
                    nc.vector.tensor_tensor(xc[:, lo:hi, :], xc[:, lo:hi, :],
                                            rstd[:, 0:1, lo:hi].rearrange("p a s -> p s a").to_broadcast([P, SPC, CH]),
                                            ALU.mult).then_inc(xn_ready, 1)

            def multiply_lr(c):
                for h in range(2):
                    j = 2 * c + h
                    s = slice(c * SPC + h * SPC // 2, c * SPC + (h + 1) * SPC // 2)
                    lo = 2 + 2 * (j % 3)
                    src = bank[:, lo:lo + 2].rearrange("p b (s f) -> p (b s) f", f=4 * CH)
                    dve.wait_ge(lr_sig, j + 1)
                    nc.vector.tensor_tensor(lr[:, :, s].rearrange("p f s -> p s f"), src[:, :, 2 * CH:4 * CH],
                                            sig_lr[:, j % 3].rearrange("p (s f) -> p s f", f=2 * CH),
                                            ALU.mult).then_inc(lr_ready, 1)

            nc.vector.memset(eps[:], EPS).then_inc(eps_set, 1)
            mean_of(0)
            mean_of(1)
            variance1(0)
            inverse1(0)
            dve.wait_ge(w_in, 16)
            dve.wait_ge(consts, 5)
            nc.vector.tensor_tensor(
                lr_blk[:].rearrange("p g m c -> p g m c"),
                w_rep[:, 0:4 * CH].rearrange("p (a m c) -> p a m c", a=1, m=4).to_broadcast([P, GRP, 4, CH]),
                mask[:].rearrange("p g (a c) -> p g a c", a=1).to_broadcast([P, GRP, 4, CH]),
                ALU.mult).then_inc(ctr_ready, 1)
            variance1(1)
            inverse1(1)
            mean_of(2)
            nc.vector.scalar_tensor_tensor(out=center_blk[:], in0=mask[:].rearrange("p g c -> p (g c)"),
                                           scalar=-1.0 / CH, in1=ident[:], op0=ALU.mult,
                                           op1=ALU.add).then_inc(ctr_ready, 1)
            nc.vector.tensor_scalar(out0_scaled[:], mat("out0"), vec("ln2_w"), None, ALU.mult).then_inc(oscaled, 1)
            mean_of(3)
            variance1(2)
            inverse1(2)
            link(nc.vector.tensor_reduce(wout_mean[:], mat("wout"), AX.X, ALU.add))
            link(nc.vector.tensor_scalar(wout_mean[:], wout_mean[:], 1.0 / CH, None, ALU.mult))
            nc.vector.tensor_scalar(wout_c[:], mat("wout"), wout_mean[:], None, ALU.subtract).then_inc(dvw, 1)
            variance1(3)
            inverse1(3)
            for c in range(CHUNKS):
                if c < 2:
                    mean_of(4 + c)
                multiply_lr(c)
                if c < 2:
                    variance1(4 + c)
                if c == 1:
                    inverse1(4)
                if c == 0:
                    dve.wait_ge(wprod, 1)
                    nc.vector.tensor_tensor(out0_blk[:].rearrange("p (g c) -> p g c", g=GRP),
                                            bank[:, 7, 0:CH].rearrange("p (a c) -> p a c", a=1).to_broadcast([P, GRP, CH]),
                                            mask[:], ALU.mult).then_inc(out0_ready, 1)
                    nc.vector.tensor_copy(q_bias[:], bank[:, 7, CH:CH + 1]).then_inc(out0_ready, 1)
                if c == 6:
                    dve.wait_ge(r_in, 16)
                    link(nc.vector.tensor_reduce(bo_mean[:], row_rep[:, 2, :], AX.X, ALU.add))
                    link(nc.vector.tensor_scalar(bo_mean[:], bo_mean[:], 1.0 / CH, None, ALU.mult))
                    link(nc.vector.tensor_scalar(bo_c[:, 0], row_rep[:, 2, :], bo_mean[:], None, ALU.subtract))
                    for i in range(3):
                        link(nc.vector.tensor_copy(bo_part[:, i], bo_c[:, i]))
                        if i < 2:
                            link(nc.vector.tensor_tensor(bo_c[:, i + 1], bo_c[:, i], bo_part[:, i], ALU.subtract))
                    for i in range(3):
                        g = slice(i * CH, (i + 1) * CH)
                        nc.vector.tensor_copy(bo_rows[g], bo_part[g, i:i + 1, :].to_broadcast([CH, SPC, CH])
                                              ).then_inc(dvw, 1)

            for b in range(1, 8):
                dve.wait_ge(p_ready, b + 1)
                prev = p_sb[:, 0:4, :] if b == 1 else acc_p[:]
                link(nc.vector.tensor_tensor(acc_p[:], prev, p_sb[:, 4 * b:4 * b + 4, :], ALU.add))
                if b > POOL_SQ:
                    dve.wait_ge(psq_ready, b + 1)
                    prev = p_sq[:, 4 * POOL_SQ:4 * POOL_SQ + 4, :] if b == POOL_SQ + 1 else acc_q[:, 1]
                    link(nc.vector.tensor_tensor(acc_q[:, 1], prev, p_sq[:, 4 * b:4 * b + 4, :], ALU.add))
            link(nc.vector.tensor_tensor(acc_p[:, 0:2], acc_p[:, 0:2], acc_p[:, 2:4], ALU.add))
            link(nc.vector.tensor_tensor(acc_p[:, 0], acc_p[:, 0], acc_p[:, 1], ALU.add))
            link(nc.vector.tensor_tensor(acc_p[:, 1], acc_p[:, 0], acc_p[:, 0], ALU.mult))
            dve.wait_ge(accq_pool, 1)
            link(nc.vector.tensor_tensor(acc_q[:, 0], acc_q[:, 0], acc_q[:, 1], ALU.add))
            link(nc.vector.tensor_tensor(acc_q[:, 0, 0:2], acc_q[:, 0, 0:2], acc_q[:, 0, 2:4], ALU.add))
            link(nc.vector.tensor_tensor(acc_q[:, 0, 0], acc_q[:, 0, 0], acc_q[:, 0, 1], ALU.add))
            nc.vector.scalar_tensor_tensor(out=st[:, 1], in0=acc_p[:, 1], scalar=-1.0 / CH, in1=acc_q[:, 0, 0],
                                           op0=ALU.mult, op1=ALU.add).then_inc(var2, 1)
            dve.wait_ge(root2, 1)
            two = 2 * SPC
            nc.vector.reciprocal(rstd[:, 1, 0:two], std[:, 1, 0:two]).then_inc(rstd2, 1)
            dve.wait_ge(rstd2, 1)
            nc.vector.tensor_tensor(t_tok[:, 0], p_sb[:, :, 0:SPC].rearrange("p e s -> p s e"),
                                    rstd[:, 1:2, 0:SPC].rearrange("p a s -> p s a").to_broadcast([P, SPC, CH]),
                                    ALU.mult).then_inc(t0_ready, 1)
            nc.vector.reciprocal(rstd[:, 1, two:P], std[:, 1, two:P]).then_inc(rstd2, 1)

            def residual0(c):
                dve.wait_ge(q_ps, c + 1)
                dve.wait_ge(g_ready, c + 1)
                link(nc.vector.scalar_tensor_tensor(out=u[:, c % 2], in0=bank[:, Q], scalar=q_bias[:], in1=gT[:, c],
                                                    op0=ALU.add, op1=ALU.mult))
                dve.wait_ge(xT_ps, c + 1)
                if c >= 3:
                    dve.wait_ge(y_ps, c - 2)
                for j in range(BLK):
                    b = slice(j * P, (j + 1) * P)
                    nc.vector.scalar_tensor_tensor(out=x1T[:, c % 3, b], in0=bank[:, XT, b], scalar=0.0,
                                                   in1=u[:, c % 2, b], op0=ALU.add, op1=ALU.add,
                                                   accum_out=x1_sum[:, c, j:j + 1]).then_inc(x1_ready, 1)

            def gated1(c):
                dve.wait_ge(l_ps, c + 1)
                dve.wait_ge(sig1_ready, c + 1)
                if c >= 2:
                    dve.wait_ge(oT_ready, c - 1)
                nc.vector.scalar_tensor_tensor(out=o_a[:, c % 2], in0=bank[:, L], scalar=leq_bias[:],
                                               in1=sig1[:, c % 2], op0=ALU.add, op1=ALU.mult).then_inc(oa_ready, 1)

            def variance3(c):
                s = slice(c * SPC, (c + 1) * SPC)
                dve.wait_ge(ysq_ready, c + 1)
                nc.vector.tensor_reduce(st[:, 2, s], sq[:, s, :], AX.X, ALU.add).then_inc(var3, 1)

            def inverse3(b):
                lo, hi = ROOTS3[b][0] * SPC, ROOTS3[b][1] * SPC
                dve.wait_ge(root3, b + 1)
                nc.vector.reciprocal(rstd[:, 2, lo:hi], std[:, 2, lo:hi]).then_inc(rstd3, 1)

            def scale3(c):
                s = slice(c * SPC, (c + 1) * SPC)
                dve.wait_ge(rstd3, next(n for n, (lo, hi) in enumerate(ROOTS3) if lo <= c < hi) + 1)
                dve.wait_ge(y_ready, c + 1)
                link(nc.vector.tensor_tensor(yn[:, s, :], y[:, s, :],
                                             rstd[:, 2:3, s].rearrange("p a s -> p s a").to_broadcast([P, SPC, CH]),
                                             ALU.mult))
                nc.vector.tensor_tensor(yn[:, s, :], yn[:, s, :], row_rep[:, 0:1, :].to_broadcast([P, SPC, CH]),
                                        ALU.mult).then_inc(scaled, 1)

            dve.wait_ge(out0_ready, 2)
            for i in range(CHUNKS + 2):
                if 0 <= i - 1 < CHUNKS:
                    residual0(i - 1)
                if 0 <= i - 2 < CHUNKS:
                    gated1(i - 2)
                if 0 <= i - 4 < CHUNKS:
                    variance3(i - 4)
                if i == 7:
                    inverse3(0)
                for c in FINAL_AT.get(i, []):
                    scale3(c)
            inverse3(1)
            variance3(6)
            scale3(4)
            inverse3(2)
            scale3(5)
            variance3(7)
            scale3(6)
            inverse3(3)
            scale3(7)

        @block.tensor
        def _(pe):
            def transpose_xn(c):
                if c < OWN_CENTRE:
                    pe.wait_ge(xn_ready, c + 1)
                else:
                    pe.wait_ge(xn_pool, c + 1 - OWN_CENTRE)
                if c >= 2:
                    pe.wait_ge(xnT_ready, c - 1)
                for j in range(BLK):
                    s = c * SPC + j * GRP
                    last = nc.tensor.transpose(bank[:, c % 2, j * P:(j + 1) * P],
                                               xc[:, s:s + GRP, :].rearrange("p s c -> p (s c)"), ident[:])
                last.then_inc(xnT_ps, 1)

            def project_lr(c):
                pe.wait_ge(xnT_ready, c + 1)
                for h in range(2):
                    j = 2 * c + h
                    if j >= 3:
                        pe.wait_ge(lr_ready, j - 2)
                    for n in range(2):
                        k = 2 * h + n
                        last = nc.tensor.matmul(bank[:, 2 + 2 * (j % 3) + n], xnT[:, c, k * P:(k + 1) * P],
                                                lr_blk[:].rearrange("p g m c -> p (g m c)"), start=True, stop=True)
                    last.then_inc(lr_ps, 1)

            pe.wait_ge(consts, 5)
            transpose_xn(0)
            pe.wait_ge(ctr_ready, 2)
            pe.wait_ge(oscaled, 1)
            nc.tensor.matmul(bank[:, 7, 0:CH], center_blk[:], out0_scaled[:], start=True, stop=True)
            pe.wait_ge(blks, 1)
            nc.tensor.matmul(bank[:, 7, CH:CH + 1], out0_raw_blk[:], vec("ln2_b"), start=True, stop=True
                             ).then_inc(wprod, 1)
            transpose_xn(1)
            for c in range(CHUNKS):
                if c == 1:
                    pe.wait_ge(out0_ready, 2)
                project_lr(c)
                if c + 2 < CHUNKS:
                    transpose_xn(c + 2)

            pe.wait_ge(lr_ready, 2 * CHUNKS)
            pe.wait_ge(xnT_ready, CHUNKS)
            for e in range(CH):
                last = nc.tensor.matmul(bank[:, e // 4, (e % 4) * P:(e % 4 + 1) * P], lr[:, e, :], lr[:, CH + e, :],
                                        start=True, stop=True)
                if e % 4 == 3:
                    last.then_inc(tri_ps, 1)

            pe.wait_ge(blks, 2)
            for c in range(CHUNKS):
                pe.wait_ge(psq_ready, c + 1)
                nc.tensor.matmul(bank[:, c], gate0_blk[:], xnT[:, c], start=True, stop=True).then_inc(g_ps, 1)

            def transpose_t(c):
                if c == 0:
                    pe.wait_ge(t0_ready, 1)
                else:
                    pe.wait_ge(t_ready, c)
                pe.wait_ge(tT_ready, c) if c else pe.wait_ge(g_ready, TT + 1)
                for j in range(BLK):
                    last = nc.tensor.transpose(bank[:, TT, j * P:(j + 1) * P],
                                               t_tok[:, c % 2, j * GRP:(j + 1) * GRP, :].rearrange("p s c -> p (s c)"),
                                               ident[:])
                last.then_inc(tT_ps, 1)

            def project_q(c):
                pe.wait_ge(tT_ready, c + 1)
                if c:
                    pe.wait_ge(x1_ready, BLK * c)
                else:
                    pe.wait_ge(g_ready, XT + 1)
                nc.tensor.matmul(bank[:, Q], out0_blk[:], tT[:, c % 2], start=True, stop=True).then_inc(q_ps, 1)
                for j in range(BLK):
                    s = c * SPC + j * GRP
                    last = nc.tensor.transpose(bank[:, XT, j * P:(j + 1) * P],
                                               x_tok[:, s:s + GRP, :].rearrange("p s c -> p (s c)"), ident[:])
                last.then_inc(xT_ps, 1)

            def project_1(c):
                pe.wait_ge(x1_ready, BLK * (c + 1))
                pe.wait_ge(rs_ready, c) if c else pe.wait_ge(g_ready, RS + 1)
                nc.tensor.matmul(bank[:, RS, 0:BLK], right_blk[:], x1_sum[:, c], start=True, stop=True
                                 ).then_inc(rs_ps, 1)
                if c:
                    pe.wait_ge(sig1_ready, c)
                nc.tensor.matmul(bank[:, G], gate1_blk[:], x1T[:, c % 3], start=True, stop=True).then_inc(g1_ps, 1)
                if c:
                    pe.wait_ge(oa_ready, c)
                nc.tensor.matmul(bank[:, L], leq_blk[:], x1T[:, c % 3], start=True, stop=True).then_inc(l_ps, 1)

            def project_y(c):
                b = Y + c % 2
                if c >= 2:
                    pe.wait_ge(y_ready, c - 1)
                elif c == 0:
                    pe.wait_ge(g_ready, CHUNKS)
                nc.tensor.matmul(bank[:, b], ones_rows[:], bo_rows[:].rearrange("p s c -> p (s c)"),
                                 start=True, stop=False, skip_group_check=True)
                for j in range(BLK):
                    k = slice(j * P, (j + 1) * P)
                    nc.tensor.matmul(bank[:, b, k], x1T[:, c % 3, k], center_blk[:], start=False, stop=False,
                                     skip_group_check=True)
                pe.wait_ge(oT_ready, c + 1)
                for j in range(BLK):
                    k = slice(j * P, (j + 1) * P)
                    last = nc.tensor.matmul(bank[:, b, k], oT[:, c % 2, k], wout_blk[:], start=False,
                                            stop=j == BLK - 1, skip_group_check=True)
                last.then_inc(y_ps, 1)

            pe.wait_ge(blks, 6)
            pe.wait_ge(dvw, 4)
            pe.wait_ge(consts, 9)
            for i in range(CHUNKS + 3):
                if i < CHUNKS:
                    transpose_t(i)
                if 0 <= i - 1 < CHUNKS:
                    project_q(i - 1)
                if 0 <= i - 2 < CHUNKS:
                    project_1(i - 2)
                if 0 <= i - 3 < CHUNKS:
                    project_y(i - 3)


def kernel(**inputs):
    import numpy as _np
    import concourse.bacc as _bacc
    from concourse import mybir as _mybir
    from concourse.bass_utils import run_bass_kernel_spmd as _run

    a = {k: _np.asarray(v) for k, v in inputs.items()}
    mats = [a["L0_conv_" + n] for n in ("left1", "right1", "left2", "right2", "gate", "out_w")]
    mats += [a["L1_conv_W_" + n] for n in ("left", "eq", "gate", "right", "out")]
    vecs = [a["L0_conv_" + n] for n in ("ln1_w", "ln1_b", "ln2_w", "ln2_b")]
    vecs += [a["L1_conv_b_" + n] for n in ("left", "eq", "right", "gate")]
    rows = [a["L1_conv_ln_scale"], a["L1_conv_ln_bias"], a["L1_conv_b_out"]]
    arrays = {
        "in_x": _np.ascontiguousarray(a["x"]),
        "in_weights": _np.concatenate(mats + [v[:, None] for v in vecs], axis=1),
        "in_rows": _np.stack(rows),
    }
    nc = _bacc.Bacc("TRN2", target_bir_lowering=False, num_devices=1)
    args = [nc.dram_tensor(n, v.shape, _mybir.dt.from_np(v.dtype), kind="ExternalInput").ap()
            for n, v in arrays.items()]
    args.append(nc.dram_tensor("out", a["x"].shape, _mybir.dt.float32, kind="ExternalOutput").ap())
    pair_layers(nc, *args)
    r = _run(nc, [arrays], core_ids=[0])
    return r.results[0]["out"]
```

```python
import concourse.bass as bass
from concourse import mybir
from contextlib import ExitStack

P = 128
CH = 32
GRP = P // CH
CHUNKS = 8
SPC = P // CHUNKS
COLS = SPC * CH
BLK = COLS // P
EPS = 1e-5

MATS = ["left1", "right1", "left2", "right2", "gate0", "out0", "wleft", "weq", "wgate", "wright", "wout"]
VECS = ["ln1_w", "ln1_b", "ln2_w", "ln2_b", "b_left", "b_eq", "b_right", "b_gate", "b_out"]
ROWS = ["ln_scale", "ln_bias"]

SUMS1 = [(0, 8), (8, 16), (16, 32), (32, 48), (48, 64), (64, 96), (96, 112), (112, 128)]
ROOTS1 = [(0, 8), (8, 16), (16, 32), (32, 48), (48, 64), (64, 96), (96, 128)]
TURNS = [(0, 8), (8, 16)] + [(16 * n, 16 * n + 16) for n in range(1, 8)]
OWN_CENTRE = 1
ROOTS3 = [(0, 2), (2, 4), (4, 6), (6, 7), (7, 8)]


def holding(ranges, s):
    return next(n for n, (lo, hi) in enumerate(ranges) if lo <= s < hi)


SCALE_AT = {6: [0], 7: [1], 8: [2], 9: [3]}
BIAS_AT = {7: [0], 8: [1], 9: [2, 3]}
ROOT3_AT = {5: 0, 7: 1, 9: 2}
WARM_UP = 10
SPLIT_FROM = 2
LOW_POOL = [2, 3]
LOW_DVE = [c for c in range(SPLIT_FROM, CHUNKS) if c not in LOW_POOL]
FIRST2 = 3 * SPC
GATE0_BANK = [0, 1, 3, 4, 5, 6, 7, 3]
GATES_FIRST = 2
POOL_SQ = 5


def pair_layers(nc, x, weights, rows, out):
    fp32, fp32r = mybir.dt.float32, mybir.dt.float32r
    ALU, ACT, AX = mybir.AluOpType, mybir.ActivationFunctionType, mybir.AxisListType

    x_tok_dram = x[0].rearrange("s r c -> r s c")
    out_tok_dram = out[0].rearrange("s r c -> r s c")
    n_w = weights.shape[1]

    with ExitStack() as ctx:
        def sb(name, shape, dt=fp32):
            return ctx.enter_context(nc.sbuf_tensor(name, shape, dt))

        def sem(name):
            return ctx.enter_context(nc.semaphore(name))

        w_rep = sb("w_rep", [P, n_w])
        row_rep = sb("row_rep", [P, len(ROWS), CH])
        mask = sb("mask", [P, GRP, CH])
        ident = sb("ident", [P, P])
        center_blk = sb("center_blk", [P, P])
        lr_blk = sb("lr_blk", [P, GRP, 4, CH])
        lr_high = sb("lr_high", [P, GRP, 4, CH], fp32r)
        lr_low = sb("lr_low", [P, GRP, 4, CH], fp32r)
        gate0_blk = sb("gate0_blk", [P, P])
        out0_raw_blk = sb("out0_raw_blk", [P, P])
        out0_scaled = sb("out0_scaled", [P, CH])
        out0_blk = sb("out0_blk", [P, P])
        q_bias = sb("q_bias", [P, 1])
        leq = sb("leq", [P, CH])
        leq_blk = sb("leq_blk", [P, P])
        center_scaled = sb("center_scaled", [P, P])
        wout_scaled = sb("wout_scaled", [P, P])
        leq_bias = sb("leq_bias", [P, 1])
        gate1_bias = sb("gate1_bias", [P, 1])
        gate1_blk = sb("gate1_blk", [P, P])
        proj_high = sb("proj_high", [P, 2, P], fp32r)
        proj_low = sb("proj_low", [P, 2, P], fp32r)
        right_blk = sb("right_blk", [P, P])
        right_bias = sb("right_bias", [P, 1])
        wout_mean = sb("wout_mean", [P, 1])
        wout_c = sb("wout_c", [P, CH])
        wout_blk = sb("wout_blk", [P, P])

        x_tok = sb("x_tok", [P, P, CH])
        xc = sb("xc", [P, P, CH])
        sq = sb("sq", [P, P, CH])
        xnT = sb("xnT", [P, CHUNKS, COLS])
        xn_high = sb("xn_high", [P, 3, COLS], fp32r)
        xn_low = sb("xn_low", [P, 3, COLS], fp32r)
        sig_lr = sb("sig_lr", [P, 3, 2 * COLS // 2])
        lr = sb("lr", [P, 2 * CH, P])
        p_sb = sb("p_sb", [P, CH, P])
        acc_p = sb("acc_p", [P, 4, P])
        acc_q = sb("acc_q", [P, 2, 4, P])
        gT = sb("gT", [P, CHUNKS, COLS])
        st = sb("st", [P, 3, P])
        mean = sb("mean", [P, 4, P])
        std = sb("std", [P, 3, P])
        rstd = sb("rstd", [P, 3, P])
        eps = sb("eps", [P, 1])
        scratch = sb("scratch", [P, 1])
        t_tok = sb("t_tok", [P, 2, SPC, CH])
        tT = sb("tT", [P, 2, COLS])
        u = sb("u", [P, 2, COLS])
        x1T = sb("x1T", [P, 3, COLS])
        x1_high, x1_low = xn_high, xn_low
        x1_sum = sb("x1_sum", [P, CHUNKS, BLK])
        rsum = sb("rsum", [P, CHUNKS, BLK])
        sig1 = sb("sig1", [P, 2, COLS])
        o_a = sb("o_a", [P, 2, COLS])
        oT = sb("oT", [P, 2, COLS])
        p_sq = sq[:].rearrange("p s c -> p (s c)").rearrange("p (e s) -> p e s", s=P)
        y = lr[:, 0:CH, :].rearrange("p f s -> p (f s)").rearrange("p (s c) -> p s c", c=CH)
        yn = lr[:, CH:2 * CH, :].rearrange("p f s -> p (f s)").rearrange("p (s c) -> p s c", c=CH)

        bank = ctx.enter_context(nc.psum_tensor("bank", [P, 8, COLS], fp32))

        def vec(name):
            i = len(MATS) * CH + VECS.index(name)
            return w_rep[:, i:i + 1]

        def mat(name):
            i = MATS.index(name) * CH
            return w_rep[:, i:i + CH]

        x_in = [sem(f"x_in{b}") for b in range(len(SUMS1))]
        w_in, r_in, x_out = sem("w_in"), sem("r_in"), sem("x_out")
        zeroed, consts, blks, dvw, wstep = sem("zeroed"), sem("consts"), sem("blks"), sem("dvw"), sem("wstep")
        ctr_ready, oscaled, wprod, out0_ready = sem("ctr_ready"), sem("oscaled"), sem("wprod"), sem("out0_ready")
        mean1, centred1_pool, squared1 = sem("mean1"), sem("centred1_pool"), sem("squared1")
        var1, root1, rstd1, xn_ready, xn_pool = sem("var1"), sem("root1"), sem("rstd1"), sem("xn_ready"), sem("xn_pool")
        lr_blk_ready, centre0, less_ready = sem("lr_blk_ready"), sem("centre0"), sem("less_ready")
        step, eps_set, warm = sem("step"), sem("eps_set"), sem("warm")
        proj_split, x1_high_ready, x1_low_ready = sem("proj_split"), sem("x1_high_ready"), sem("x1_low_ready")
        lr_high_ready = sem("lr_high_ready")
        lr_split, xn_high_ready = sem("lr_split"), sem("xn_high_ready")
        xn_low_pool, xn_low_dve = sem("xn_low_pool"), sem("xn_low_dve")
        bo_ps, biases = sem("bo_ps"), sem("biases")
        xnT_ps, xnT_ready = sem("xnT_ps"), sem("xnT_ready")
        lr_ps, lr_sig, lr_ready = sem("lr_ps"), sem("lr_sig"), sem("lr_ready")
        tri_ps, p_ready, psq_ready = sem("tri_ps"), sem("p_ready"), sem("psq_ready")
        accq_pool, var2, root2, rstd2 = sem("accq_pool"), sem("var2"), sem("root2"), sem("rstd2")
        pool_step = sem("pool_step")
        g_ps, g_ready = sem("g_ps"), sem("g_ready")
        t0_ready, t_ready, tT_ps, tT_ready = sem("t0_ready"), sem("t_ready"), sem("tT_ps"), sem("tT_ready")
        q_ps, xT_ps, u_ready, x1_ready = sem("q_ps"), sem("xT_ps"), sem("u_ready"), sem("x1_ready")
        rs_ps, rs_ready, l_ps, g1_ps, sig1_ready = (
            sem("rs_ps"), sem("rs_ready"), sem("l_ps"), sem("g1_ps"), sem("sig1_ready"))
        oa_ready, oT_ready = sem("oa_ready"), sem("oT_ready")
        y_ps, y_ready, ysq_ready, yn_ready = sem("y_ps"), sem("y_ready"), sem("ysq_ready"), sem("yn_ready")
        var3, root3, rstd3 = sem("var3"), sem("root3"), sem("rstd3")
        out_scaled, ys_ps = sem("out_scaled"), sem("ys_ps")
        last_half, half_out = sem("last_half"), sem("half_out")
        scaled, final = sem("scaled"), sem("final")

        TT, Q, XT, L, G, RS, Y = 0, 1, 2, 3, 4, 5, 6
        SCALED = Q

        def low_bits(engine, c, done):
            return engine.tensor_tensor(xn_low[:, c % 3], xnT[:, c], xn_high[:, c % 3],
                                        ALU.subtract).then_inc(done, 1)

        block = ctx.enter_context(nc.Block())

        @block.sync
        def _(sp):
            for b, (lo, hi) in enumerate(SUMS1):
                sp.dma_start(x_tok[:, lo:hi, :], x_tok_dram[:, lo:hi, :]).then_inc(x_in[b], 16)
            for c in range(CHUNKS - 1):
                s = slice(c * SPC, (c + 1) * SPC)
                sp.wait_ge(final, c + 1)
                sp.dma_start(out_tok_dram[:, s, :], sq[:, s, :]).then_inc(x_out, 16)
            s = slice(P - SPC // 2, P)
            sp.wait_ge(last_half, 2)
            sp.dma_start(out_tok_dram[:, s, :], sq[:, s, :]).then_inc(x_out, 16)
            sp.wait_ge(x_out, 16 * CHUNKS)

        @block.gpsimd
        def _(pool):
            nc.gpsimd.memset(mask[:], 0.0).then_inc(zeroed, 1)
            nc.gpsimd.memset(ident[:], 0.0).then_inc(zeroed, 1)
            pool.wait_ge(zeroed, 2)
            nc.gpsimd.affine_select(out=ident[:], in_=ident[:], compare_op=ALU.not_equal, fill=1.0,
                                    base=0, pattern=[[-1, P]], channel_multiplier=1).then_inc(consts, 1)
            for g in range(GRP):
                pool.wait_ge(consts, 1 + g)
                nc.gpsimd.memset(mask[g * CH:(g + 1) * CH, g, :], 1.0).then_inc(consts, 1)

            def center(b):
                lo, hi = SUMS1[b]
                pool.wait_ge(mean1, b + 1)
                nc.gpsimd.tensor_tensor(xc[:, lo:hi, :], x_tok[:, lo:hi, :],
                                        mean[:, 0:1, lo:hi].rearrange("p a s -> p s a").to_broadcast([P, hi - lo, CH]),
                                        ALU.subtract).then_inc(centred1_pool, 1)

            def normalise1(n):
                lo, hi = TURNS[n]
                pool.wait_ge(rstd1, holding(ROOTS1, lo) + 1)
                pool.wait_ge(centred1_pool, holding(SUMS1, lo) + 1 - OWN_CENTRE)
                nc.gpsimd.tensor_tensor(xc[:, lo:hi, :], xc[:, lo:hi, :],
                                        rstd[:, 0:1, lo:hi].rearrange("p a s -> p s a").to_broadcast([P, hi - lo, CH]),
                                        ALU.mult).then_inc(xn_pool, 1)

            def block_diagonal(dst, src):
                nc.gpsimd.tensor_tensor(dst.rearrange("p (g c) -> p g c", g=GRP),
                                        src.rearrange("p (a c) -> p a c", a=1).to_broadcast([P, GRP, CH]),
                                        mask[:], ALU.mult).then_inc(blks, 1)

            def low(c):
                pool.wait_ge(xn_high_ready, c - SPLIT_FROM + 1)
                low_bits(nc.gpsimd, c, xn_low_pool)

            pool.wait_ge(consts, 5)
            pool.wait_ge(w_in, 16)
            nc.gpsimd.tensor_scalar(out0_scaled[:], mat("out0"), vec("ln2_w"), None, ALU.mult).then_inc(oscaled, 1)
            block_diagonal(out0_raw_blk[:], mat("out0"))
            nc.gpsimd.tensor_tensor(lr_blk[:],
                                    w_rep[:, 0:4 * CH].rearrange("p (a m c) -> p a m c", a=1, m=4)
                                    .to_broadcast([P, GRP, 4, CH]),
                                    mask[:].rearrange("p g (a c) -> p g a c", a=1).to_broadcast([P, GRP, 4, CH]),
                                    ALU.mult).then_inc(lr_blk_ready, 1)
            center(1)
            for b in range(2, 6):
                center(b)
                normalise1(b - 1)
            normalise1(5)
            normalise1(6)
            low(2)
            low(3)
            for b in (6, 7):
                center(b)
            for n in (7, 8):
                normalise1(n)
            block_diagonal(gate0_blk[:], mat("gate0"))
            nc.gpsimd.tensor_tensor(leq[:], mat("wleft"), mat("weq"), ALU.add).then_inc(pool_step, 1)
            nc.gpsimd.tensor_tensor(leq_bias[:], vec("b_left"), vec("b_eq"), ALU.add).then_inc(pool_step, 1)
            pool.wait_ge(pool_step, 2)
            block_diagonal(leq_blk[:], leq[:])
            block_diagonal(gate1_blk[:], mat("wgate"))
            block_diagonal(right_blk[:], mat("wright"))
            pool.wait_ge(dvw, 1)
            block_diagonal(wout_blk[:], wout_c[:])

            pool.wait_ge(r_in, 16)
            pool.wait_ge(blks, 6)
            for dst, blk in ((center_scaled, center_blk), (wout_scaled, wout_blk)):
                nc.gpsimd.tensor_tensor(dst[:].rearrange("p (g c) -> p g c", g=GRP),
                                        blk[:].rearrange("p (g c) -> p g c", g=GRP),
                                        row_rep[:, 0:1, :].to_broadcast([P, GRP, CH]), ALU.mult).then_inc(out_scaled, 1)
            for n, blk in enumerate((leq_blk, gate1_blk)):
                nc.gpsimd.tensor_copy(proj_high[:, n], blk[:]).then_inc(proj_split, 1)
            pool.wait_ge(proj_split, 2)
            for n, blk in enumerate((leq_blk, gate1_blk)):
                nc.gpsimd.tensor_tensor(proj_low[:, n], blk[:], proj_high[:, n], ALU.subtract).then_inc(proj_split, 1)

            for b in range(1, POOL_SQ):
                pool.wait_ge(psq_ready, b + 1)
                if b > 1:
                    pool.wait_ge(pool_step, 2 + b - 1)
                prev = p_sq[:, 0:4, :] if b == 1 else acc_q[:, 0]
                nc.gpsimd.tensor_tensor(acc_q[:, 0], prev, p_sq[:, 4 * b:4 * b + 4, :],
                                        ALU.add).then_inc(pool_step if b < POOL_SQ - 1 else accq_pool, 1)

            def normalise2(c):
                s = slice(c * SPC, (c + 1) * SPC)
                pool.wait_ge(rstd2, 1 if c * SPC < FIRST2 else 2)
                if c >= 2:
                    pool.wait_ge(tT_ps, c - 1)
                nc.gpsimd.tensor_tensor(t_tok[:, c % 2], p_sb[:, :, s].rearrange("p e s -> p s e"),
                                        rstd[:, 1:2, s].rearrange("p a s -> p s a").to_broadcast([P, SPC, CH]),
                                        ALU.mult).then_inc(t_ready, 1)

            def low1(c):
                pool.wait_ge(x1_high_ready, c + 1)
                if c >= 2:
                    pool.wait_ge(l_ps, c - 1)
                nc.gpsimd.tensor_tensor(x1_low[:, c % 2], x1T[:, c % 3], x1_high[:, c % 2],
                                        ALU.subtract).then_inc(x1_low_ready, 1)

            def times_right(c):
                pool.wait_ge(oa_ready, c + 1)
                pool.wait_ge(rs_ready, c // 2 + 1)
                if c >= 2:
                    pool.wait_ge(y_ps, c - 1)
                nc.gpsimd.tensor_tensor(oT[:, c % 2].rearrange("p (b k) -> p b k", b=BLK),
                                        o_a[:, c % 2].rearrange("p (b k) -> p b k", b=BLK),
                                        rsum[:, c:c + 1, :].rearrange("p a b -> p b a").to_broadcast([P, BLK, P]),
                                        ALU.mult).then_inc(oT_ready, 1)

            def bias3(c):
                s = slice(c * SPC, (c + 1) * SPC)
                pool.wait_ge(scaled, c + 1)
                nc.gpsimd.tensor_tensor(sq[:, s, :], yn[:, s, :], row_rep[:, 1:2, :].to_broadcast([P, SPC, CH]),
                                        ALU.add).then_inc(final, 1)

            normalise2(1)
            for i in range(CHUNKS + 2):
                if i >= 3 and i % 2:
                    times_right(i - 3)
                if 0 <= i - 1 < CHUNKS:
                    low1(i - 1)
                if i >= 3 and i % 2:
                    times_right(i - 2)
                if i + 2 < CHUNKS:
                    normalise2(i + 2)
                for c in BIAS_AT.get(i, []):
                    bias3(c)
            for c in range(4, CHUNKS - 1):
                bias3(c)

        @block.scalar
        def _(act):
            act.dma_start(w_rep[:], weights.rearrange("(a p) n -> a p n", a=1).to_broadcast([GRP, CH, n_w])
                          ).then_inc(w_in, 16)
            act.dma_start(row_rep[:], rows.rearrange("(a v) c -> a v c", a=1).to_broadcast([P, len(ROWS), CH])
                          ).then_inc(r_in, 16)

            def square1(b):
                lo, hi = SUMS1[b]
                act.wait_ge(x_in[b], 16)
                nc.scalar.activation(sq[:, lo:hi, :], x_tok[:, lo:hi, :], ACT.Square).then_inc(squared1, 1)

            def root(layer, lo, hi, done):
                nc.scalar.activation(std[:, layer, lo:hi], st[:, layer, lo:hi], ACT.Sqrt, scale=1.0 / CH,
                                     bias=eps[:]).then_inc(done, 1)

            def root1_of(b):
                lo, hi = ROOTS1[b]
                act.wait_ge(var1, holding(SUMS1, hi - 1) + 1)
                root(0, lo, hi, root1)

            def affine1(n):
                lo, hi = TURNS[n]
                c, cols = lo // SPC, slice(lo % SPC * CH, ((hi - 1) % SPC + 1) * CH)
                act.wait_ge(xnT_ps, n + 1)
                nc.scalar.activation(xnT[:, c, cols], bank[:, n % 2, cols], ACT.Identity, bias=vec("ln1_b"),
                                     scale=vec("ln1_w")).then_inc(xnT_ready, 1)
                if c >= SPLIT_FROM:
                    act.wait_ge(xnT_ready, n + 1)
                    nc.scalar.activation(xn_high[:, c % 3], xnT[:, c], ACT.Copy).then_inc(xn_high_ready, 1)

            def sigmoid_lr(c, h):
                j = 2 * c + h
                act.wait_ge(lr_ps, j + 1)
                if j >= 3:
                    act.wait_ge(lr_ready, j - 2)
                lo = 2 + 2 * (j % 3)
                src = bank[:, lo:lo + 2].rearrange("p b (s f) -> p (b s) f", f=4 * CH)
                nc.scalar.activation(sig_lr[:, j % 3].rearrange("p (s f) -> p s f", f=2 * CH),
                                     src[:, :, 0:2 * CH], ACT.Sigmoid).then_inc(lr_sig, 1)

            act.wait_ge(eps_set, 1)
            nc.scalar.activation(std[:, 0, 0:1], eps[:], ACT.Sqrt).then_inc(warm, 1)
            act.wait_ge(warm, 1)
            square1(0)
            square1(1)
            root1_of(0)
            square1(2)
            act.wait_ge(w_in, 16)
            affine1(0)
            root1_of(1)
            square1(3)
            root1_of(2)
            square1(4)
            affine1(1)
            root1_of(3)
            square1(5)
            act.wait_ge(lr_blk_ready, 1)
            nc.scalar.activation(lr_high[:], lr_blk[:], ACT.Copy).then_inc(lr_high_ready, 1)
            affine1(2)
            root1_of(4)
            square1(6)
            root1_of(5)
            for c in range(CHUNKS):
                sigmoid_lr(c, 0)
                if c == 0:
                    affine1(3)
                elif c < CHUNKS - 2:
                    affine1(c + 3)
                sigmoid_lr(c, 1)
                if c == 0:
                    square1(7)
                if c == 2:
                    root1_of(6)

            for b in range(8):
                act.wait_ge(tri_ps, b + 1)
                src = bank[:, b].rearrange("p (e s) -> p e s", e=4)
                nc.scalar.activation(p_sb[:, 4 * b:4 * b + 4, :], src, ACT.Copy).then_inc(p_ready, 1)
                nc.scalar.activation(p_sq[:, 4 * b:4 * b + 4, :], src, ACT.Square).then_inc(psq_ready, 1)

            def gate0(c):
                act.wait_ge(g_ps, c + 1)
                nc.scalar.activation(gT[:, c], bank[:, GATE0_BANK[c]], ACT.Sigmoid).then_inc(g_ready, 1)

            for c in range(GATES_FIRST):
                gate0(c)
            act.wait_ge(var2, 1)
            root(1, 0, FIRST2, root2)

            def evacuate_tT(c):
                act.wait_ge(tT_ps, c + 1)
                if c >= 2:
                    act.wait_ge(q_ps, c - 1)
                nc.scalar.activation(tT[:, c % 2], bank[:, TT], ACT.Copy).then_inc(tT_ready, 1)

            def high1(c):
                act.wait_ge(x1_ready, BLK * (c + 1))
                if c >= 2:
                    act.wait_ge(l_ps, c - 1)
                nc.scalar.activation(x1_high[:, c % 2], x1T[:, c % 3], ACT.Copy).then_inc(x1_high_ready, 1)

            def sums_of_right(m):
                act.wait_ge(rs_ps, m + 1)
                nc.scalar.activation(rsum[:, 2 * m:2 * m + 2].rearrange("p c b -> p (c b)"),
                                     bank[:, RS, 0:2 * BLK], ACT.Identity,
                                     bias=right_bias[:]).then_inc(rs_ready, 1)

            def gate1(c):
                act.wait_ge(g1_ps, c + 1)
                if c >= 2:
                    act.wait_ge(oa_ready, c - 1)
                nc.scalar.activation(sig1[:, c % 2], bank[:, G], ACT.Sigmoid, bias=gate1_bias[:]
                                     ).then_inc(sig1_ready, 1)

            def evacuate_y(c):
                s = slice(c * SPC, (c + 1) * SPC)
                src = bank[:, Y + c % 2].rearrange("p (s c) -> p s c", c=CH)
                act.wait_ge(y_ps, c + 1)
                nc.scalar.activation(sq[:, s, :], src, ACT.Square).then_inc(ysq_ready, 1)
                nc.scalar.activation(y[:, s, :], src, ACT.Copy).then_inc(y_ready, 1)

            def root3_of(b):
                act.wait_ge(var3, ROOTS3[b][1])
                root(2, ROOTS3[b][0] * SPC, ROOTS3[b][1] * SPC, root3)

            for i in range(CHUNKS + 3):
                if i < CHUNKS:
                    evacuate_tT(i)
                if i == 0:
                    act.wait_ge(var2, 2)
                    root(1, FIRST2, P, root2)
                if i == 1:
                    for c in range(GATES_FIRST, 5):
                        gate0(c)
                if i == 2:
                    for c in range(5, CHUNKS):
                        gate0(c)
                    act.wait_ge(biases, 3)
                if i >= 3 and i % 2 and i - 2 < CHUNKS:
                    sums_of_right((i - 3) // 2)
                if 0 <= i - 1 < CHUNKS:
                    high1(i - 1)
                if 0 <= i - 2 < CHUNKS:
                    gate1(i - 2)
                if i in ROOT3_AT:
                    root3_of(ROOT3_AT[i])
                if 0 <= i - 3 < CHUNKS:
                    evacuate_y(i - 3)
                if i in ROOT3_AT and i <= CHUNKS:
                    nc.scalar.activation(scratch[:], eps[:], ACT.Sigmoid)
            root3_of(3)
            root3_of(4)
            s = slice(P - SPC, P - SPC // 2)
            act.wait_ge(last_half, 1)
            act.dma_start(out_tok_dram[:, s, :], sq[:, s, :]).then_inc(half_out, 16)
            act.wait_ge(half_out, 16)

        @block.vector
        def _(dve):
            steps = [0]

            def link(instruction):
                steps[0] += 1
                instruction.then_inc(step, 1)
                dve.wait_ge(step, steps[0])

            def variance1(b):
                lo, hi = SUMS1[b]
                sums, less, squares = mean[:, 1, lo:hi], mean[:, 2, lo:hi], mean[:, 3, lo:hi]
                dve.wait_ge(x_in[b], 16)
                link(nc.vector.tensor_reduce(sums, x_tok[:, lo:hi, :], AX.X, ALU.add))
                nc.vector.tensor_scalar(mean[:, 0, lo:hi], sums, 1.0 / CH, None, ALU.mult).then_inc(mean1, 1)
                nc.vector.scalar_tensor_tensor(out=less, in0=sums, scalar=-1.0 / CH, in1=sums, op0=ALU.mult,
                                               op1=ALU.mult).then_inc(less_ready, 1)
                dve.wait_ge(squared1, b + 1)
                link(nc.vector.tensor_reduce(squares, sq[:, lo:hi, :], AX.X, ALU.add))
                dve.wait_ge(less_ready, b + 1)
                nc.vector.tensor_tensor(st[:, 0, lo:hi], squares, less, ALU.add).then_inc(var1, 1)

            def inverse1(b):
                lo, hi = ROOTS1[b]
                dve.wait_ge(root1, b + 1)
                nc.vector.reciprocal(rstd[:, 0, lo:hi], std[:, 0, lo:hi]).then_inc(rstd1, 1)
                if b < OWN_CENTRE:
                    dve.wait_ge(rstd1, b + 1)
                    dve.wait_ge(centre0, b + 1)
                    nc.vector.tensor_tensor(xc[:, lo:hi, :], xc[:, lo:hi, :],
                                            rstd[:, 0:1, lo:hi].rearrange("p a s -> p s a").to_broadcast([P, hi - lo, CH]),
                                            ALU.mult).then_inc(xn_ready, 1)

            def multiply_lr(c, h):
                j = 2 * c + h
                s = slice(c * SPC + h * SPC // 2, c * SPC + (h + 1) * SPC // 2)
                lo = 2 + 2 * (j % 3)
                src = bank[:, lo:lo + 2].rearrange("p b (s f) -> p (b s) f", f=4 * CH)
                dve.wait_ge(lr_sig, j + 1)
                nc.vector.tensor_tensor(lr[:, :, s].rearrange("p f s -> p s f"), src[:, :, 2 * CH:4 * CH],
                                        sig_lr[:, j % 3].rearrange("p (s f) -> p s f", f=2 * CH),
                                        ALU.mult).then_inc(lr_ready, 1)

            nc.vector.memset(eps[:], EPS).then_inc(eps_set, 1)
            dve.wait_ge(consts, 5)
            nc.vector.scalar_tensor_tensor(out=center_blk[:], in0=mask[:].rearrange("p g c -> p (g c)"),
                                           scalar=-1.0 / CH, in1=ident[:], op0=ALU.mult,
                                           op1=ALU.add).then_inc(ctr_ready, 1)
            variance1(0)
            lo, hi = SUMS1[0]
            nc.vector.tensor_tensor(xc[:, lo:hi, :], x_tok[:, lo:hi, :],
                                    mean[:, 0:1, lo:hi].rearrange("p a s -> p s a").to_broadcast([P, hi - lo, CH]),
                                    ALU.subtract).then_inc(centre0, 1)
            inverse1(0)
            variance1(1)
            variance1(2)
            inverse1(1)
            dve.wait_ge(wprod, 1)
            nc.vector.tensor_tensor(out0_blk[:].rearrange("p (g c) -> p g c", g=GRP),
                                    bank[:, 7, 0:CH].rearrange("p (a c) -> p a c", a=1).to_broadcast([P, GRP, CH]),
                                    mask[:], ALU.mult).then_inc(out0_ready, 1)
            nc.vector.tensor_copy(q_bias[:], bank[:, 7, CH:CH + 1]).then_inc(out0_ready, 1)
            inverse1(2)
            variance1(3)
            variance1(4)
            inverse1(3)
            variance1(5)
            inverse1(4)
            dve.wait_ge(lr_high_ready, 1)
            nc.vector.tensor_tensor(lr_low[:], lr_blk[:], lr_high[:], ALU.subtract).then_inc(lr_split, 1)
            inverse1(5)
            for c in range(CHUNKS):
                multiply_lr(c, 0)
                if c + 2 in LOW_DVE:
                    dve.wait_ge(xn_high_ready, c + 2 - SPLIT_FROM + 1)
                    low_bits(nc.vector, c + 2, xn_low_dve)
                if c == 1:
                    variance1(6)
                multiply_lr(c, 1)
                if c == 1:
                    variance1(7)
                if c == 2:
                    inverse1(6)
                if c == 2:
                    dve.wait_ge(w_in, 16)
                    link(nc.vector.tensor_reduce(wout_mean[:], mat("wout"), AX.X, ALU.add))
                    link(nc.vector.tensor_scalar(wout_mean[:], wout_mean[:], 1.0 / CH, None, ALU.mult))
                    nc.vector.tensor_scalar(wout_c[:], mat("wout"), wout_mean[:], None, ALU.subtract).then_inc(dvw, 1)
            dve.wait_ge(bo_ps, 1)
            dve.wait_ge(blks, 5)
            nc.vector.tensor_tensor(leq_bias[:], leq_bias[:], bank[:, 1, 0:1], ALU.subtract).then_inc(biases, 1)
            nc.vector.tensor_tensor(gate1_bias[:], vec("b_gate"), bank[:, 1, 1:2], ALU.subtract).then_inc(biases, 1)
            link(nc.vector.tensor_tensor(right_bias[:], vec("b_right"), bank[:, 1, 2:3], ALU.subtract))
            nc.vector.tensor_scalar(right_bias[:], right_bias[:], float(P), None, ALU.mult).then_inc(biases, 1)

            def tick(instruction):
                steps[0] += 1
                instruction.then_inc(step, 1)
                return steps[0]

            for b in range(1, 7):
                dve.wait_ge(p_ready, b + 1)
                prev = p_sb[:, 0:4, :] if b == 1 else acc_p[:]
                link(nc.vector.tensor_tensor(acc_p[:], prev, p_sb[:, 4 * b:4 * b + 4, :], ALU.add))
                if b > POOL_SQ:
                    dve.wait_ge(psq_ready, b + 1)
                    prev = p_sq[:, 4 * POOL_SQ:4 * POOL_SQ + 4, :] if b == POOL_SQ + 1 else acc_q[:, 1]
                    link(nc.vector.tensor_tensor(acc_q[:, 1], prev, p_sq[:, 4 * b:4 * b + 4, :], ALU.add))

            def add_last_p(s):
                return tick(nc.vector.tensor_tensor(acc_p[:, :, s], acc_p[:, :, s], p_sb[:, 28:32, s], ALU.add))

            def variance2(s, p):
                q = tick(nc.vector.tensor_tensor(acc_q[:, 1, :, s], acc_q[:, 1, :, s], p_sq[:, 28:32, s], ALU.add))
                dve.wait_ge(step, p)
                p = tick(nc.vector.tensor_tensor(acc_p[:, 0:2, s], acc_p[:, 0:2, s], acc_p[:, 2:4, s], ALU.add))
                dve.wait_ge(step, q)
                q = tick(nc.vector.tensor_tensor(acc_q[:, 0, :, s], acc_q[:, 0, :, s], acc_q[:, 1, :, s], ALU.add))
                dve.wait_ge(step, p)
                p = tick(nc.vector.tensor_tensor(acc_p[:, 0, s], acc_p[:, 0, s], acc_p[:, 1, s], ALU.add))
                dve.wait_ge(step, q)
                q = tick(nc.vector.tensor_tensor(acc_q[:, 0, 0:2, s], acc_q[:, 0, 0:2, s], acc_q[:, 0, 2:4, s],
                                                 ALU.add))
                dve.wait_ge(step, p)
                p = tick(nc.vector.tensor_tensor(acc_p[:, 1, s], acc_p[:, 0, s], acc_p[:, 0, s], ALU.mult))
                dve.wait_ge(step, q)
                q = tick(nc.vector.tensor_tensor(acc_q[:, 0, 0, s], acc_q[:, 0, 0, s], acc_q[:, 0, 1, s], ALU.add))
                dve.wait_ge(step, q)
                nc.vector.scalar_tensor_tensor(out=st[:, 1, s], in0=acc_p[:, 1, s], scalar=-1.0 / CH,
                                               in1=acc_q[:, 0, 0, s], op0=ALU.mult, op1=ALU.add).then_inc(var2, 1)

            first, rest = slice(0, FIRST2), slice(FIRST2, P)
            dve.wait_ge(p_ready, 8)
            p = add_last_p(first)
            dve.wait_ge(psq_ready, 8)
            dve.wait_ge(accq_pool, 1)
            variance2(first, p)
            p = add_last_p(rest)
            dve.wait_ge(root2, 1)
            nc.vector.reciprocal(rstd[:, 1, first], std[:, 1, first]).then_inc(rstd2, 1)
            dve.wait_ge(rstd2, 1)
            nc.vector.tensor_tensor(t_tok[:, 0], p_sb[:, :, 0:SPC].rearrange("p e s -> p s e"),
                                    rstd[:, 1:2, 0:SPC].rearrange("p a s -> p s a").to_broadcast([P, SPC, CH]),
                                    ALU.mult).then_inc(t0_ready, 1)
            variance2(rest, p)
            dve.wait_ge(root2, 2)
            nc.vector.reciprocal(rstd[:, 1, rest], std[:, 1, rest]).then_inc(rstd2, 1)

            def residual0(c):
                dve.wait_ge(q_ps, c + 1)
                dve.wait_ge(g_ready, c + 1)
                link(nc.vector.scalar_tensor_tensor(out=u[:, c % 2], in0=bank[:, Q], scalar=q_bias[:], in1=gT[:, c],
                                                    op0=ALU.add, op1=ALU.mult))
                dve.wait_ge(xT_ps, c + 1)
                if c >= 3:
                    dve.wait_ge(y_ps, c - 2)
                for j in range(BLK):
                    b = slice(j * P, (j + 1) * P)
                    nc.vector.scalar_tensor_tensor(out=x1T[:, c % 3, b], in0=bank[:, XT, b], scalar=vec("b_out"),
                                                   in1=u[:, c % 2, b], op0=ALU.add, op1=ALU.add,
                                                   accum_out=x1_sum[:, c, j:j + 1]).then_inc(x1_ready, 1)

            def gated1(c):
                dve.wait_ge(l_ps, c + 1)
                dve.wait_ge(sig1_ready, c + 1)
                if c >= 2:
                    dve.wait_ge(oT_ready, c - 1)
                nc.vector.scalar_tensor_tensor(out=o_a[:, c % 2], in0=bank[:, L], scalar=leq_bias[:],
                                               in1=sig1[:, c % 2], op0=ALU.add, op1=ALU.mult).then_inc(oa_ready, 1)

            def variance3(c):
                s = slice(c * SPC, (c + 1) * SPC)
                dve.wait_ge(ysq_ready, c + 1)
                nc.vector.tensor_reduce(st[:, 2, s], sq[:, s, :], AX.X, ALU.add).then_inc(var3, 1)

            def inverse3(b):
                lo, hi = ROOTS3[b][0] * SPC, ROOTS3[b][1] * SPC
                dve.wait_ge(root3, b + 1)
                nc.vector.reciprocal(rstd[:, 2, lo:hi], std[:, 2, lo:hi]).then_inc(rstd3, 1)

            def scale3(c):
                s, n = slice(c * SPC, (c + 1) * SPC), SPC
                dve.wait_ge(rstd3, next(n for n, (lo, hi) in enumerate(ROOTS3) if lo <= c < hi) + 1)
                dve.wait_ge(y_ready, c + 1)
                link(nc.vector.tensor_tensor(yn[:, s, :], y[:, s, :],
                                             rstd[:, 2:3, s].rearrange("p a s -> p s a").to_broadcast([P, n, CH]),
                                             ALU.mult))
                nc.vector.tensor_tensor(yn[:, s, :], yn[:, s, :], row_rep[:, 0:1, :].to_broadcast([P, n, CH]),
                                        ALU.mult).then_inc(scaled, 1)

            def normalise3(c, lo, hi):
                dve.wait_ge(ys_ps, c - CHUNKS + 3)
                src = bank[:, SCALED + c % 2].rearrange("p (s c) -> p s c", c=CH)[:, lo - c * SPC:hi - c * SPC, :]
                nc.vector.tensor_tensor(yn[:, lo:hi, :], src,
                                        rstd[:, 2:3, lo:hi].rearrange("p a s -> p s a").to_broadcast([P, hi - lo, CH]),
                                        ALU.mult).then_inc(scaled, 1)

            dve.wait_ge(out0_ready, 2)
            for i in range(CHUNKS + 2):
                if 0 <= i - 1 < CHUNKS:
                    residual0(i - 1)
                if i <= CHUNKS:
                    for c in SCALE_AT.get(i, []):
                        scale3(c)
                if 0 <= i - 4 < CHUNKS:
                    variance3(i - 4)
                if 0 <= i - 2 < CHUNKS:
                    gated1(i - 2)
                if i > CHUNKS:
                    for c in SCALE_AT.get(i, []):
                        scale3(c)
                if i in ROOT3_AT:
                    inverse3(ROOT3_AT[i])
            scale3(4)
            variance3(6)
            scale3(5)
            inverse3(3)
            variance3(7)
            dve.wait_ge(rstd3, len(ROOTS3) - 1)
            normalise3(6, 6 * SPC, 7 * SPC)
            inverse3(4)
            lo = (CHUNKS - 1) * SPC
            dve.wait_ge(rstd3, len(ROOTS3))
            for h in (lo, lo + SPC // 2):
                normalise3(7, h, h + SPC // 2)
            for n, h in enumerate((lo, lo + SPC // 2)):
                dve.wait_ge(scaled, CHUNKS + n)
                nc.vector.tensor_tensor(sq[:, h:h + SPC // 2, :], yn[:, h:h + SPC // 2, :],
                                        row_rep[:, 1:2, :].to_broadcast([P, SPC // 2, CH]), ALU.add
                                        ).then_inc(last_half, 1)

        @block.tensor
        def _(pe):
            def transpose_xn(n):
                lo, hi = TURNS[n]
                if n < OWN_CENTRE:
                    pe.wait_ge(xn_ready, n + 1)
                else:
                    pe.wait_ge(xn_pool, n + 1 - OWN_CENTRE)
                if n >= 2:
                    pe.wait_ge(xnT_ready, n - 1)
                for s in range(lo, hi, GRP):
                    k = s % SPC * CH
                    last = nc.tensor.transpose(bank[:, n % 2, k:k + P],
                                               xc[:, s:s + GRP, :].rearrange("p s c -> p (s c)"), ident[:])
                last.then_inc(xnT_ps, 1)

            def project_lr(c, h):
                j = 2 * c + h
                pe.wait_ge(xnT_ready, holding(TURNS, 8 * j) + 1)
                if j >= 3:
                    pe.wait_ge(lr_ready, j - 2)
                if j == 2 * SPLIT_FROM:
                    pe.wait_ge(lr_split, 1)
                if c in LOW_POOL:
                    pe.wait_ge(xn_low_pool, LOW_POOL.index(c) + 1)
                elif c in LOW_DVE:
                    pe.wait_ge(xn_low_dve, LOW_DVE.index(c) + 1)
                for n in range(2):
                    if j == 1 and n == 1:
                        transpose_xn(2)
                    k = 2 * h + n
                    b, cols = 2 + 2 * (j % 3) + n, slice(k * P, (k + 1) * P)
                    if c < SPLIT_FROM:
                        last = nc.tensor.matmul(bank[:, b], xnT[:, c, cols],
                                                lr_blk[:].rearrange("p g m c -> p (g m c)"), start=True, stop=True)
                        continue
                    high, low = (w[:].rearrange("p g m c -> p (g m c)") for w in (lr_high, lr_low))
                    nc.tensor.matmul(bank[:, b], xn_high[:, c % 3, cols], high, start=True, stop=False)
                    nc.tensor.matmul(bank[:, b], xn_high[:, c % 3, cols], low, start=False, stop=False)
                    last = nc.tensor.matmul(bank[:, b], xn_low[:, c % 3, cols], high, start=False, stop=True)
                last.then_inc(lr_ps, 1)

            pe.wait_ge(consts, 5)
            for _ in range(WARM_UP):
                nc.tensor.matmul(bank[:, 6, 0:P], ident[:], ident[:], start=True, stop=True)
            pe.wait_ge(ctr_ready, 1)
            pe.wait_ge(oscaled, 1)
            nc.tensor.matmul(bank[:, 7, 0:CH], center_blk[:], out0_scaled[:], start=True, stop=True)
            pe.wait_ge(blks, 1)
            nc.tensor.matmul(bank[:, 7, CH:CH + 1], out0_raw_blk[:], vec("ln2_b"), start=True, stop=True
                             ).then_inc(wprod, 1)
            transpose_xn(0)
            pe.wait_ge(lr_blk_ready, 1)
            for c in range(CHUNKS):
                if c == 1:
                    pe.wait_ge(out0_ready, 2)
                project_lr(c, 0)
                if c == 0:
                    transpose_xn(1)
                elif c < CHUNKS - 2:
                    transpose_xn(c + 3)
                project_lr(c, 1)
                if c == 0:
                    transpose_xn(3)

            pe.wait_ge(blks, 6)
            pe.wait_ge(xnT_ready, len(TURNS))
            for n, blk in enumerate((leq_blk, gate1_blk, right_blk)):
                last = nc.tensor.matmul(bank[:, 1, n:n + 1], blk[:], vec("b_out"), start=True, stop=True)
            last.then_inc(bo_ps, 1)

            pe.wait_ge(lr_ready, 2 * CHUNKS)
            for e in range(CH):
                if e == 4:
                    pe.wait_ge(biases, 3)
                last = nc.tensor.matmul(bank[:, e // 4, (e % 4) * P:(e % 4 + 1) * P], lr[:, e, :], lr[:, CH + e, :],
                                        start=True, stop=True)
                if e % 4 == 3:
                    last.then_inc(tri_ps, 1)

            def project_gate0(c):
                b = GATE0_BANK[c]
                pe.wait_ge(psq_ready, b + 1)
                if b in GATE0_BANK[:c]:
                    pe.wait_ge(g_ready, GATE0_BANK.index(b) + 1)
                nc.tensor.matmul(bank[:, b], gate0_blk[:], xnT[:, c], start=True, stop=True).then_inc(g_ps, 1)

            def transpose_x(c):
                if c:
                    pe.wait_ge(x1_ready, BLK * c)
                else:
                    pe.wait_ge(psq_ready, XT + 1)
                for j in range(BLK):
                    s = c * SPC + j * GRP
                    last = nc.tensor.transpose(bank[:, XT, j * P:(j + 1) * P],
                                               x_tok[:, s:s + GRP, :].rearrange("p s c -> p (s c)"), ident[:])
                last.then_inc(xT_ps, 1)

            for c in range(6):
                project_gate0(c)
                if c == 3:
                    transpose_x(0)

            def transpose_t(c):
                if c == 0:
                    pe.wait_ge(t0_ready, 1)
                else:
                    pe.wait_ge(t_ready, c)
                pe.wait_ge(tT_ready, c) if c else pe.wait_ge(g_ready, TT + 1)
                for j in range(BLK):
                    last = nc.tensor.transpose(bank[:, TT, j * P:(j + 1) * P],
                                               t_tok[:, c % 2, j * GRP:(j + 1) * GRP, :].rearrange("p s c -> p (s c)"),
                                               ident[:])
                last.then_inc(tT_ps, 1)

            def project_q(c):
                pe.wait_ge(tT_ready, c + 1)
                if c:
                    pe.wait_ge(x1_ready, BLK * c - 3)
                else:
                    pe.wait_ge(g_ready, Q + 1)
                nc.tensor.matmul(bank[:, Q], out0_blk[:], tT[:, c % 2], start=True, stop=True).then_inc(q_ps, 1)
                if c:
                    transpose_x(c)

            def project_sums(m):
                pe.wait_ge(x1_ready, 2 * BLK * (m + 1))
                pe.wait_ge(rs_ready, m) if m else pe.wait_ge(g_ready, GATE0_BANK.index(RS) + 1)
                nc.tensor.matmul(bank[:, RS, 0:2 * BLK], right_blk[:],
                                 x1_sum[:, 2 * m:2 * m + 2].rearrange("p c b -> p (c b)"), start=True, stop=True
                                 ).then_inc(rs_ps, 1)

            def project_split(c, b, n, done):
                nc.tensor.matmul(bank[:, b], proj_high[:, n], x1_high[:, c % 2], start=True, stop=False)
                nc.tensor.matmul(bank[:, b], proj_low[:, n], x1_high[:, c % 2], start=False, stop=False)
                pe.wait_ge(x1_low_ready, c + 1)
                nc.tensor.matmul(bank[:, b], proj_high[:, n], x1_low[:, c % 2], start=False, stop=True
                                 ).then_inc(done, 1)

            def project_1(c):
                pe.wait_ge(x1_high_ready, c + 1)
                if c:
                    pe.wait_ge(sig1_ready, c)
                else:
                    pe.wait_ge(proj_split, 4)
                project_split(c, G, 1, g1_ps)
                if c:
                    pe.wait_ge(oa_ready, c)
                else:
                    pe.wait_ge(g_ready, CHUNKS)
                project_split(c, L, 0, l_ps)

            def center_y(c):
                b = Y + c % 2
                if c >= 2:
                    pe.wait_ge(y_ready, c - 1)
                elif c == 0:
                    pe.wait_ge(g_ready, CHUNKS)
                for j in range(BLK):
                    k = slice(j * P, (j + 1) * P)
                    nc.tensor.matmul(bank[:, b, k], x1T[:, c % 3, k], center_blk[:], start=j == 0, stop=False,
                                     skip_group_check=True)

            def project_y(c):
                b = Y + c % 2
                pe.wait_ge(oT_ready, c + 1)
                for j in range(BLK):
                    k = slice(j * P, (j + 1) * P)
                    last = nc.tensor.matmul(bank[:, b, k], oT[:, c % 2, k], wout_blk[:], start=False,
                                            stop=j == BLK - 1, skip_group_check=True)
                last.then_inc(y_ps, 1)

            def project_scaled(c):
                for n, (lhs, rhs) in enumerate(((x1T[:, c % 3], center_scaled), (oT[:, c % 2], wout_scaled))):
                    for j in range(BLK):
                        k = slice(j * P, (j + 1) * P)
                        last = nc.tensor.matmul(bank[:, SCALED + c % 2, k], lhs[:, k], rhs[:],
                                                start=n == 0 and j == 0, stop=n == 1 and j == BLK - 1,
                                                skip_group_check=True)
                last.then_inc(ys_ps, 1)

            for i in range(CHUNKS + 3):
                if i < CHUNKS:
                    transpose_t(i)
                if i == 0:
                    project_gate0(6)
                if 0 <= i - 1 < CHUNKS:
                    project_q(i - 1)
                if i == 2:
                    project_gate0(7)
                if i >= 3 and i % 2 and i - 2 < CHUNKS:
                    project_sums((i - 3) // 2)
                if 0 <= i - 3 < CHUNKS:
                    center_y(i - 3)
                if 0 <= i - 2 < CHUNKS:
                    project_1(i - 2)
                if 0 <= i - 3 < CHUNKS:
                    project_y(i - 3)
            pe.wait_ge(out_scaled, 2)
            pe.wait_ge(x1_ready, BLK * CHUNKS)
            project_scaled(CHUNKS - 2)
            project_scaled(CHUNKS - 1)


def kernel(**inputs):
    import numpy as _np
    import concourse.bacc as _bacc
    from concourse import mybir as _mybir
    from concourse.bass_utils import run_bass_kernel_spmd as _run

    a = {k: _np.asarray(v) for k, v in inputs.items()}
    mats = [a["L0_conv_" + n] for n in ("left1", "right1", "left2", "right2", "gate", "out_w")]
    mats += [a["L1_conv_W_" + n] for n in ("left", "eq", "gate", "right", "out")]
    vecs = [a["L0_conv_" + n] for n in ("ln1_w", "ln1_b", "ln2_w", "ln2_b")]
    vecs += [a["L1_conv_b_" + n] for n in ("left", "eq", "right", "gate", "out")]
    rows = [a["L1_conv_ln_scale"], a["L1_conv_ln_bias"]]
    arrays = {
        "in_x": _np.ascontiguousarray(a["x"]),
        "in_weights": _np.concatenate(mats + [v[:, None] for v in vecs], axis=1),
        "in_rows": _np.stack(rows),
    }
    nc = _bacc.Bacc("TRN2", target_bir_lowering=False, num_devices=1)
    args = [nc.dram_tensor(n, v.shape, _mybir.dt.from_np(v.dtype), kind="ExternalInput").ap()
            for n, v in arrays.items()]
    args.append(nc.dram_tensor("out", a["x"].shape, _mybir.dt.float32, kind="ExternalOutput").ap())
    pair_layers(nc, *args)
    r = _run(nc, [arrays], core_ids=[0])
    return r.results[0]["out"]
```
